# Optimizing a Trainium2 kernel written in Bass

```python
import numpy as np
import jax
import jax.numpy as jnp

def _softmax(x, axis=-1):
    return jax.nn.softmax(x, axis=axis)

def _gelu(x):
    return jax.nn.gelu(x, approximate=True)

def _silu(x):
    return jax.nn.silu(x)

def _sigmoid(x):
    return jax.nn.sigmoid(x)

def _layernorm(x, axis=-1, eps=1e-05):
    m = jnp.mean(x, axis=axis, keepdims=True)
    v = jnp.var(x, axis=axis, keepdims=True)
    return (x - m) / jnp.sqrt(v + eps)

def _scatter_add(tgt, idx, src, axis=0):
    return tgt.at[idx].add(src)

def _segment_sum(src, seg, n):
    return jax.ops.segment_sum(src, seg, n)
kernel_name = 'mk_adaln_ffn_d2_seqx_r8_ae1ce8'

def setup_inputs(seed: int=0):
    np.random.seed(seed)
    _w = jnp.asarray

    def _rec_inputs():
        import jax
        import jax.numpy as jnp
        _rk = jax.random.key(seed)
        x = -0.000125 + 0.9999 * jax.random.normal(jax.random.fold_in(_rk, 1), (64, 32, 512), jnp.float32)
        _lenS = 32 - jax.random.randint(jax.random.fold_in(_rk, 7), (64,), 0, max(1, 32 // 4) + 1, jnp.int32)
        _lenS2 = 32 - jax.random.randint(jax.random.fold_in(_rk, 8), (64,), 0, max(1, 32 // 4) + 1, jnp.int32)
        cond_128 = 0.0061147 + 1.02565 * jax.random.normal(jax.random.fold_in(_rk, 11), (64, 128), jnp.float32)
        fside_S_0 = -0.022604 + 0.987366 * jax.random.normal(jax.random.fold_in(_rk, 12), (32,), jnp.float32)
        return (x, cond_128, fside_S_0)
    x, cond_128, fside_S_0 = _rec_inputs()

    def _L0_cond_setup():
        import jax, jax.numpy as jnp
        import numpy as np
        K = 8
        T = 1.0
        D_EMBD = 128
        IN_C = 32
        OUT_C = 32
        BS = 32
        H = 512
        HID = 128
        key = jax.random.key(seed)
        ks = jax.random.split(key, 10)
        s = lambda fan_in: 1.0 / np.sqrt(fan_in)
        return {'x': jax.random.normal(ks[0], (BS, IN_C, H), dtype=jnp.float32), 'embedding': jax.random.normal(ks[1], (BS, D_EMBD), dtype=jnp.float32), 'W0': jax.random.normal(ks[2], (D_EMBD, HID), dtype=jnp.float32) * s(D_EMBD), 'b0': jnp.zeros((HID,), dtype=jnp.float32), 'W1': jax.random.normal(ks[3], (HID, HID), dtype=jnp.float32) * s(HID), 'b1': jnp.zeros((HID,), dtype=jnp.float32), 'W2': jax.random.normal(ks[4], (HID, K), dtype=jnp.float32) * s(HID), 'b2': jnp.zeros((K,), dtype=jnp.float32), 'weight': jax.random.normal(ks[5], (K, OUT_C, IN_C, 1), dtype=jnp.float32) * s(IN_C), 'bias_k': jax.random.normal(ks[6], (K, OUT_C), dtype=jnp.float32) * 0.1}
    _L0_cond_all = _L0_cond_setup()
    _L0_cond_in = {k: v for k, v in _L0_cond_all.items() if k in ('W0', 'b0', 'W1', 'b1', 'W2', 'b2', 'weight', 'bias_k')}
    del _L0_cond_all

    def _L0_ffn_setup():
        import jax, jax.numpy as jnp
        import numpy as np
        H = 512
        I = 1376
        R = 32
        NLEV = 16
        Q_ZERO = 7.5
        Q_STEP = 0.005
        LR_SCALE = 0.02

        def _qlinear(x, q, scale, A, Bm):
            w = (q.astype(jnp.float32) - Q_ZERO) * (scale * Q_STEP)[:, None]
            y = jnp.einsum('bsh,oh->bso', x, w)
            return y + LR_SCALE * (x @ A @ Bm)
        key = jax.random.key(seed)
        ks = jax.random.split(key, 13)
        B, S = (2, 256)
        inp = {'x': jax.random.normal(ks[0], (B, S, H), jnp.float32), 'gate_q': jax.random.randint(ks[1], (I, H), 0, NLEV, jnp.int32), 'gate_scale': jax.random.uniform(ks[2], (I,), jnp.float32), 'gate_A': jax.random.normal(ks[3], (H, R), jnp.float32), 'gate_B': jax.random.normal(ks[4], (R, I), jnp.float32), 'up_q': jax.random.randint(ks[5], (I, H), 0, NLEV, jnp.int32), 'up_scale': jax.random.uniform(ks[6], (I,), jnp.float32), 'up_A': jax.random.normal(ks[7], (H, R), jnp.float32), 'up_B': jax.random.normal(ks[8], (R, I), jnp.float32), 'down_q': jax.random.randint(ks[9], (H, I), 0, NLEV, jnp.int32), 'down_scale': jax.random.uniform(ks[10], (H,), jnp.float32), 'down_A': jax.random.normal(ks[11], (I, R), jnp.float32), 'down_B': jax.random.normal(ks[12], (R, H), jnp.float32)}
        return inp
    _L0_ffn_all = _L0_ffn_setup()
    _L0_ffn_in = {k: v for k, v in _L0_ffn_all.items() if k in ('gate_q', 'gate_scale', 'gate_A', 'gate_B', 'up_q', 'up_scale', 'up_A', 'up_B', 'down_q', 'down_scale', 'down_A', 'down_B')}
    del _L0_ffn_all

    def _L1_cond_setup():
        import jax, jax.numpy as jnp
        import numpy as np
        from jax import lax
        N, C_IN, L = (32, 32, 512)
        C_OUT, K, GROUPS = (32, 9, 4)
        C_DIM, PAD, STRIDE = (128, 4, 1)
        key = jax.random.key(seed)
        k1, k2, k3, k4, k5 = jax.random.split(key, 5)
        x = jax.random.normal(k1, (N, C_IN, L), dtype=jnp.float32)
        c = jax.random.normal(k2, (N, C_DIM), dtype=jnp.float32)
        weight = jax.random.normal(k3, (C_OUT, C_IN // GROUPS, K), dtype=jnp.float32)
        c_weight = jax.random.normal(k4, (C_OUT, C_DIM), dtype=jnp.float32)
        bias = jax.random.normal(k5, (C_OUT,), dtype=jnp.float32)
        return {'x': x, 'c': c, 'weight': weight, 'c_weight': c_weight, 'bias': bias}
    _L1_cond_all = _L1_cond_setup()
    _L1_cond_in = {k: v for k, v in _L1_cond_all.items() if k in ('weight', 'c_weight')}
    del _L1_cond_all

    def _L1_ffn_setup():
        import jax, jax.numpy as jnp
        import numpy as np
        FP8_MAX = 448.0
        K = 512
        N = 512

        def _compute_scale(t):
            amax = jnp.max(jnp.abs(t))
            return FP8_MAX / jnp.maximum(amax, 1e-12)

        def _quantize_fp8(t, scale):
            return jnp.clip(t * scale, -FP8_MAX, FP8_MAX).astype(jnp.float8_e4m3fn)
        key = jax.random.key(seed)
        kx, kw = jax.random.split(key)
        x = jax.random.normal(kx, (8, 256, K), dtype=jnp.float32)
        weight = jax.random.normal(kw, (K, N), dtype=jnp.float32) * 0.02
        return {'x': x, 'weight': weight}
    _L1_ffn_all = _L1_ffn_setup()
    _L1_ffn_in = {k: v for k, v in _L1_ffn_all.items() if k in ('weight',)}
    del _L1_ffn_all
    return {'x': x, 'cond_128': cond_128, 'fside_S_0': fside_S_0, 'L0_cond_W0': _L0_cond_in['W0'], 'L0_cond_b0': _L0_cond_in['b0'], 'L0_cond_W1': _L0_cond_in['W1'], 'L0_cond_b1': _L0_cond_in['b1'], 'L0_cond_W2': _L0_cond_in['W2'], 'L0_cond_b2': _L0_cond_in['b2'], 'L0_cond_weight': _L0_cond_in['weight'], 'L0_cond_bias_k': _L0_cond_in['bias_k'], 'L0_ffn_gate_q': _L0_ffn_in['gate_q'], 'L0_ffn_gate_scale': _L0_ffn_in['gate_scale'], 'L0_ffn_gate_A': _L0_ffn_in['gate_A'], 'L0_ffn_gate_B': _L0_ffn_in['gate_B'], 'L0_ffn_up_q': _L0_ffn_in['up_q'], 'L0_ffn_up_scale': _L0_ffn_in['up_scale'], 'L0_ffn_up_A': _L0_ffn_in['up_A'], 'L0_ffn_up_B': _L0_ffn_in['up_B'], 'L0_ffn_down_q': _L0_ffn_in['down_q'], 'L0_ffn_down_scale': _L0_ffn_in['down_scale'], 'L0_ffn_down_A': _L0_ffn_in['down_A'], 'L0_ffn_down_B': _L0_ffn_in['down_B'], 'L1_cond_weight': _L1_cond_in['weight'], 'L1_cond_c_weight': _L1_cond_in['c_weight'], 'L1_ffn_weight': _L1_ffn_in['weight']}

def reference(x, cond_128, fside_S_0, L0_cond_W0, L0_cond_b0, L0_cond_W1, L0_cond_b1, L0_cond_W2, L0_cond_b2, L0_cond_weight, L0_cond_bias_k, L0_ffn_gate_q, L0_ffn_gate_scale, L0_ffn_gate_A, L0_ffn_gate_B, L0_ffn_up_q, L0_ffn_up_scale, L0_ffn_up_A, L0_ffn_up_B, L0_ffn_down_q, L0_ffn_down_scale, L0_ffn_down_A, L0_ffn_down_B, L1_cond_weight, L1_cond_c_weight, L1_ffn_weight):
    import jax
    import jax.numpy as jnp

    def _L0_cond_ref(x, embedding, W0, b0, W1, b1, W2, b2, weight, bias_k):
        import jax, jax.numpy as jnp
        import numpy as np
        K = 8
        T = 1.0
        D_EMBD = 128
        IN_C = 32
        OUT_C = 32
        BS = 32
        H = 512
        HID = 128
        h = jax.nn.gelu(embedding @ W0 + b0, approximate=False)
        h = jax.nn.gelu(h @ W1 + b1, approximate=False)
        att = jax.nn.softmax((h @ W2 + b2) / T, axis=-1)
        agg_w = jnp.einsum('bk,koi->boi', att, weight[..., 0])
        agg_b = att @ bias_k
        out = jnp.einsum('boi,bih->boh', agg_w, x) + agg_b[:, :, None]
        return out

    def _L0_ffn_ref(x, gate_q, gate_scale, gate_A, gate_B, up_q, up_scale, up_A, up_B, down_q, down_scale, down_A, down_B):
        import jax, jax.numpy as jnp
        import numpy as np
        H = 512
        I = 1376
        R = 32
        NLEV = 16
        Q_ZERO = 7.5
        Q_STEP = 0.005
        LR_SCALE = 0.02

        def _qlinear(x, q, scale, A, Bm):
            w = (q.astype(jnp.float32) - Q_ZERO) * (scale * Q_STEP)[:, None]
            y = jnp.einsum('bsh,oh->bso', x, w)
            return y + LR_SCALE * (x @ A @ Bm)
        g = _qlinear(x, gate_q, gate_scale, gate_A, gate_B)
        u = _qlinear(x, up_q, up_scale, up_A, up_B)
        h = jax.nn.silu(g) * u
        return _qlinear(h, down_q, down_scale, down_A, down_B)

    def _L1_cond_ref(x, c, weight, c_weight, bias):
        import jax, jax.numpy as jnp
        import numpy as np
        from jax import lax
        N, C_IN, L = (32, 32, 512)
        C_OUT, K, GROUPS = (32, 9, 4)
        C_DIM, PAD, STRIDE = (128, 4, 1)
        out = lax.conv_general_dilated(x, weight, window_strides=(STRIDE,), padding=[(PAD, PAD)], dimension_numbers=('NCH', 'OIH', 'NCH'), feature_group_count=GROUPS)
        ctx = jnp.einsum('nd,od->no', c, c_weight)
        out = out + ctx[:, :, None] + bias[None, :, None]
        return out

    def _L1_ffn_ref(x, weight):
        import jax, jax.numpy as jnp
        import numpy as np
        FP8_MAX = 448.0
        K = 512
        N = 512

        def _compute_scale(t):
            amax = jnp.max(jnp.abs(t))
            return FP8_MAX / jnp.maximum(amax, 1e-12)

        def _quantize_fp8(t, scale):
            return jnp.clip(t * scale, -FP8_MAX, FP8_MAX).astype(jnp.float8_e4m3fn)
        B, S, _ = x.shape
        x2 = x.reshape(-1, K)
        x_scale = _compute_scale(x2)
        w_scale = _compute_scale(weight)
        x_fp8 = _quantize_fp8(x2, x_scale)
        w_fp8 = _quantize_fp8(weight.T, w_scale)
        out = jnp.matmul(x_fp8.astype(jnp.float32), w_fp8.T.astype(jnp.float32))
        out = out * (1.0 / x_scale * (1.0 / w_scale))
        return out.reshape(B, S, N)
    x = x + _L0_ffn_ref(_L0_cond_ref(x, cond_128, L0_cond_W0, L0_cond_b0, L0_cond_W1, L0_cond_b1, L0_cond_W2, L0_cond_b2, L0_cond_weight, L0_cond_bias_k), L0_ffn_gate_q, L0_ffn_gate_scale, L0_ffn_gate_A, L0_ffn_gate_B, L0_ffn_up_q, L0_ffn_up_scale, L0_ffn_up_A, L0_ffn_up_B, L0_ffn_down_q, L0_ffn_down_scale, L0_ffn_down_A, L0_ffn_down_B)
    x = x + _L1_ffn_ref(_L1_cond_ref(x, cond_128, L1_cond_weight, L1_cond_c_weight, fside_S_0), L1_ffn_weight)
    return x

_drawn_inputs = setup_inputs


def setup_inputs(seed=0):
    import zlib

    import numpy as np

    out = dict(_drawn_inputs(seed))
    spreads = {'L0_cond_b0': (0.0, 0.1), 'L0_cond_b1': (0.0, 0.1), 'L0_cond_b2': (0.0, 0.1)}
    factors = {}
    for name, (base, spread) in spreads.items():
        noise = np.random.default_rng([zlib.crc32(name.encode()), seed]).standard_normal(out[name].shape)
        drawn = base * np.exp(spread * noise) if base else spread * noise
        out[name] = jnp.asarray(drawn.astype(out[name].dtype))
    for name, factor in factors.items():
        out[name] = (out[name] * factor).astype(out[name].dtype)
    return out
```

```python
from contextlib import ExitStack

import concourse.bass as bass
from concourse import mybir

F32 = mybir.dt.float32
F32R = mybir.dt.float32r
BF16 = mybir.dt.bfloat16
I32 = mybir.dt.int32
U16 = mybir.dt.uint16
ACT = mybir.ActivationFunctionType
ALU = mybir.AluOpType
AX_X = mybir.AxisListType.X

P = 128
B, S, H = 64, 32, 512
TOKENS = B * S
I = 1376
R = 32
EXPERTS = 8
TAPS, PAD = 9, 4
CONV_GROUPS = 4
Q_ZERO, Q_STEP, LR_SCALE = 7.5, 0.005, 0.02
FP8_MAX, AMAX_MIN = 448.0, 1e-12

HC = H // P
IC = -(-I // P)
GROUPS = TOKENS // P
GB = P // S
TILE = 512
TILES = TOKENS // TILE
TG = TILE // P
PAIRS = B // 2
CG = S // CONV_GROUPS
RING = 8
STACKED = 3
EXP_MASK = 0x7F80
E4M3_MIN_NORMAL = 2.0 ** -6
ROUND_AT_3_BITS = 1.5 * 2.0 ** 20


COND_WIDTHS = (B, P, P, EXPERTS, 1, 1, EXPERTS)
COND_AT = tuple(sum(COND_WIDTHS[:n]) for n in range(len(COND_WIDTHS)))
COND_COLS = sum(COND_WIDTHS)
OB = P // S


def width(ic):
    return min(P, I - ic * P)


def build(nc, x, cond_pack, cond_w, bias_k, gate_q, up_q, gate_s, up_s,
          lr_a, gate_b, up_b, down_q, down_s, down_a, down_b, conv_w, ctx_w, fside, ffn_w,
          block_mask, ident_in, sel_in, out):
    with ExitStack() as ctx:
        def sb(name, shape, dt, stack=ctx):
            return stack.enter_context(nc.sbuf_tensor(name, shape, dt))

        def sem(name):
            return ctx.enter_context(nc.semaphore(name))

        ps = ctx.enter_context(nc.psum_tensor("ps", [P, 8, 512], F32))

        x_nat = sb("x_nat", [P, GROUPS, H], F32)
        conv_wt = sb("conv_wt", [P, TAPS, P], F32R)
        ctx_bias = sb("ctx_bias", [P, PAIRS], F32)
        ident = sb("ident", [P, P], F32)
        ones = sb("ones", [P, P], F32)
        y_buf = sb("y_buf", [P, 2, H], F32)
        small = sb("small", [P, 64], F32)
        amax = sb("amax", [P, GROUPS + 2], F32)
        x1_hi = sb("x1_hi", [P, HC, TILE], F32R)
        x1_lo = sb("x1_lo", [P, HC, TILE], F32R)
        down_w = sb("down_w", [P, IC, H], F32R)
        gate_b4 = sb("gate_b4", [P, I], F32R)
        up_b4 = sb("up_b4", [P, I], F32R)
        down_b4 = sb("down_b4", [P, H], F32R)
        lr_a_w = sb("lr_a_w", [P, HC, 2, 2, R], F32R)
        down_a_w = sb("down_a_w", [P, IC, 2, R], F32R)
        down_sb = sb("down_sb", [P, H], F32)
        agg_b = sb("agg_b", [P, TOKENS], F32)
        mix = sb("mix", [P, GROUPS, P], F32)
        a_buf = sb("a_buf", [P, 2, TILE], F32)
        b_buf = sb("b_buf", [P, 2, TILE], F32)
        sel = sb("sel", [P, 2, P], F32R)
        gate_sc = sb("gate_sc", [P, IC], F32)
        up_sc = sb("up_sc", [P, IC], F32)
        t_part = sb("t_part", [P, 2, R], F32)
        t_rep = sb("t_rep", [P, 2, 4, R], F32)
        t4d = sb("t4d", [P, 2, P], F32R)
        phase1 = ExitStack()
        gate_w = sb("gate_w", [P, HC * I], F32R, phase1)
        up_w = sb("up_w", [P, HC * I], F32R, phase1)
        h_hi = sb("h_hi", [P, IC, TILE], F32R, phase1)
        h_lo = sb("h_lo", [P, IC, TILE], F32R, phase1)
        phase1.close()
        early = ExitStack()
        pad_gate = sb("pad_gate", [P, 2 * HC * I], F32, early)
        cond_in_sb = sb("cond_in_sb", [P, COND_COLS], F32, early)
        h0 = sb("h0", [P, B], F32, early)
        h1 = sb("h1", [P, B], F32, early)
        logits = sb("logits", [B, EXPERTS], F32, early)
        probs = sb("probs", [B, EXPERTS], F32, early)
        att = sb("att", [B, EXPERTS], F32, early)
        att_t = sb("att_t", [EXPERTS, B], F32, early)
        stat = sb("stat", [B, 4], F32, early)
        bias_k_sb = sb("bias_k_sb", [EXPERTS, S], F32, early)
        cond_w_sb = sb("cond_w_sb", [EXPERTS, S // OB, P], F32, early)
        att_bias = sb("att_bias", [EXPERTS, B, S], F32, early)
        stage_lr_a = sb("stage_lr_a", [P, HC, 2, R], F32, early)
        stage_sel = sb("stage_sel", [P, 2, P], F32, early)
        stage_conv = sb("stage_conv", [P, TAPS, CG], F32, early)
        stage_mask = sb("stage_mask", [P, 2 * CONV_GROUPS], F32, early)
        stage_side = sb("stage_side", [P, 1], F32, early)
        stage_ctx_w = sb("stage_ctx_w", [P, S], F32, early)
        used = 4 * (COND_COLS + 2 * B + 3 * EXPERTS + B + 4 + S + S // OB * P + B * S + HC * 2 * R + 2 * P
                    + TAPS * CG + 2 * CONV_GROUPS + 1 + S)
        pad_h = sb("pad_h", [P, (4 * IC * TILE - used) // 4 + 32], F32, early)
        stage_gate_b = sb("stage_gate_b", [P, I], F32, early)
        stage_up_b = sb("stage_up_b", [P, I], F32, early)
        stage_down_b = sb("stage_down_b", [P, H], F32, early)
        stage_down_a = sb("stage_down_a", [P, IC, R], F32, early)
        early.close()
        cond_sb, w0_sb, w1_sb, w2_sb, b0_sb, b1_sb, b2_sb = (
            cond_in_sb[0:rows, COND_AT[n]:COND_AT[n] + COND_WIDTHS[n]]
            for n, rows in enumerate((P, P, P, P, P, P, B)))
        phase2 = ExitStack()
        t_t = sb("t_t", [P, HC, TOKENS], F32, phase2)
        stacked = [sb(f"stacked{n}", [P, H + 2 * PAD], F32R, phase2) for n in range(STACKED)]
        conv_part = sb("conv_part", [64, 2, H], F32, phase2)
        z_buf = sb("z_buf", [P, 2, H], F32, phase2)
        ffn_f = sb("ffn_f", [P, HC * H], F32, phase2)
        ffn_q = sb("ffn_q", [P, HC * H], BF16, phase2)
        v16 = sb("v16", [P, 2, H], BF16, phase2)
        e16 = sb("e16", [P, 2, H], BF16, phase2)
        m16 = sb("m16", [P, 2, H], BF16, phase2)
        v_plus = sb("v_plus", [P, 2, H], F32, phase2)
        q_raw = sb("q_raw", [P, 2, H], BF16, phase2)
        q_fp8 = sb("q_fp8", [P, 2, H], BF16, phase2)
        o_buf = sb("o_buf", [P, 4, H], F32, phase2)
        phase2.close()

        cond_in = sem("cond_in")
        mixw_in = sem("mixw_in")
        x_in = [sem(f"x_in{t}") for t in range(TILES)]
        lr_in = sem("lr_in")
        lrb_in = sem("lrb_in")
        scale_in = sem("scale_in")
        down_in = sem("down_in")
        conv_in = sem("conv_in")
        q_in = [sem(f"q_in{n}") for n in range(RING)]
        ffn_in = sem("ffn_in")
        out_done = [sem(f"out_done{n}") for n in range(4)]
        const_set = sem("const_set")
        mix_zero = sem("mix_zero")
        h0_mm, h0_act = sem("h0_mm"), sem("h0_act")
        h1_mm, h1_act = sem("h1_mm"), sem("h1_act")
        logit_mm = sem("logit_mm")
        soft = sem("soft")
        exp_done = sem("exp_done")
        att_tr = sem("att_tr")
        att_ready = sem("att_ready")
        mix_mm = sem("mix_mm")
        mix_ready = sem("mix_ready")
        aggb_mm, aggb_ready = sem("aggb_mm"), sem("aggb_ready")
        ctx_mm, ctx_ready = sem("ctx_mm"), sem("ctx_ready")
        q_ready = sem("q_ready")
        scale_ready = sem("scale_ready")
        lra_hi, lra_ready = sem("lra_hi"), sem("lra_ready")
        lrb_hi, lrb_ready = sem("lrb_hi"), sem("lrb_ready")
        down_hi, down_ready = sem("down_hi"), sem("down_ready")
        conv_full, conv_hi, conv_ready = sem("conv_full"), sem("conv_hi"), sem("conv_ready")
        cond_mm = sem("cond_mm")
        xs_ready = sem("xs_ready")
        x1_hi_ready, x1_lo_ready = sem("x1_hi_ready"), sem("x1_lo_ready")
        p_mm, p_hi_ready, p_lo_ready = sem("p_mm"), sem("p_hi_ready"), sem("p_lo_ready")
        sel_mm, t4_hi_ready, t4_lo_ready = sem("sel_mm"), sem("t4_hi_ready"), sem("t4_lo_ready")
        q_mm, l_mm = sem("q_mm"), sem("l_mm")
        ag_ready, au_ready = sem("ag_ready"), sem("au_ready")
        g_ready, u_ready = sem("g_ready"), sem("u_ready")
        silu_ready, h_ready = sem("silu_ready"), sem("h_ready")
        h_hi_ready, h_lo_ready = sem("h_hi_ready"), sem("h_lo_ready")
        down_mm = sem("down_mm")
        part_ready, rep_ready, rep_tr = sem("part_ready"), sem("rep_ready"), sem("rep_tr")
        t4d_hi_ready, t4d_lo_ready = sem("t4d_hi_ready"), sem("t4d_lo_ready")
        down_l_mm = sem("down_l_mm")
        yq_ready, y_ready, x2_ready = sem("yq_ready"), sem("y_ready"), sem("x2_ready")
        stack_hi_ready, stack_lo_ready = sem("stack_hi_ready"), sem("stack_lo_ready")
        conv_mm, part_out, z_ready = sem("conv_mm"), sem("part_out"), sem("z_ready")
        z_tr, tt_ready, amax_ready = sem("z_tr"), sem("tt_ready"), sem("amax_ready")
        wmax, wmax_tr, wsc_mm = sem("wmax"), sem("wmax_tr"), sem("wsc_mm")
        xmax, xmax_tr, xsc_mm = sem("xmax"), sem("xmax_tr"), sem("xsc_mm")
        scales_ready = sem("scales_ready")
        v_ready, exp_ready, m_ready = sem("v_ready"), sem("exp_ready"), sem("m_ready")
        wq_step = sem("wq_step")
        ffn_ready, v_plus_ready, q_raw_ready = sem("ffn_ready"), sem("v_plus_ready"), sem("q_raw_ready")
        q_fp8_ready = sem("q_fp8_ready")
        ffn_mm, o_ready = sem("ffn_mm"), sem("o_ready")

        slots = [("gate", ic) if m == 0 else ("up", ic) for ic in range(IC) for m in range(2)]
        slots += [("down", ic) for ic in range(IC)]

        def slot_width(n):
            kind, ic = slots[n]
            return H if kind == "down" else HC * width(ic)

        def slot(n):
            return x_nat[:, GROUPS - RING + n % RING, 0:slot_width(n)].bitcast(I32)

        def slot_dram(n):
            kind, ic = slots[n]
            a = {"gate": gate_q, "up": up_q, "down": down_q}[kind]
            return a[:, H * ic:H * ic + slot_width(n)]

        def slot_weights(n):
            kind, ic = slots[n]
            w = {"gate": gate_w[:], "up": up_w[:], "down": down_w[:].rearrange("p c n -> p (c n)")}[kind]
            return w[:, H * ic:H * ic + slot_width(n)]

        def bank(ic, n):
            return 4 * (ic % 2) + n

        split_buf = [a_buf[:, 1, :], b_buf[:, 1, :], a_buf[:, 0, :], b_buf[:, 0, :]]
        p_hi, p_lo = h_hi[:, IC - 2, :], h_lo[:, IC - 2, :]
        t4 = [h_hi[:, IC - 1, :], h_lo[:, IC - 1, :]]

        def plain(ap):
            return ap.bitcast(F32)

        def x_tile(dram, t):
            return dram[t * TILE:(t + 1) * TILE, :].rearrange("(g p) h -> p g h", p=P)

        def spread_mix(copy, q, args):
            for b in range(GB):
                src = ps[q * S:(q + 1) * S, 5, :].rearrange("p (o g b) -> p b g o", g=GROUPS, b=GB)[:, b]
                dst = mix[b * S:(b + 1) * S, :, b * S:(b + 1) * S].rearrange("p g (o q) -> p q g o", q=OB)[:, q]
                last = copy(dst, src, *args)
            return last

        block = ctx.enter_context(nc.Block())

        @block.sync
        def _(sp):
            sp.dma_start(cond_in_sb[:], cond_pack).then_inc(cond_in, 16)
            sp.dma_start(cond_w_sb[:].rearrange("k o p -> k (o p)"), cond_w).then_inc(mixw_in, 16)
            sp.dma_start(bias_k_sb[:], bias_k).then_inc(mixw_in, 16)
            sp.dma_start(ident[:], ident_in).then_inc(lr_in, 16)
            sp.dma_start(stage_sel[:].rearrange("p m q -> p (m q)"), sel_in).then_inc(lr_in, 16)
            sp.dma_start(stage_lr_a[:].rearrange("p c m r -> p (c m r)"), lr_a).then_inc(lr_in, 16)
            sp.dma_start(stage_gate_b[:], gate_b).then_inc(lrb_in, 16)
            sp.dma_start(stage_up_b[:], up_b).then_inc(lrb_in, 16)
            sp.dma_start(x_nat[:, 0:TG, :], x_tile(x, 0)).then_inc(x_in[0], 16)

            def load_slot(n):
                if n >= RING:
                    sp.wait_ge(q_ready, n - RING + 1)
                sp.dma_start(slot(n), slot_dram(n)).then_inc(q_in[n % RING], 16)

            for n in range(4):
                load_slot(n)
            sp.dma_start(gate_sc[:], gate_s).then_inc(scale_in, 16)
            sp.dma_start(up_sc[:], up_s).then_inc(scale_in, 16)
            for n in range(4, RING):
                load_slot(n)
            sp.dma_start(down_sb[:], down_s).then_inc(down_in, 16)
            sp.dma_start(stage_down_a[:].rearrange("p c r -> p (c r)"), down_a).then_inc(down_in, 16)
            sp.dma_start(stage_down_b[:], down_b).then_inc(down_in, 16)
            sp.dma_start(stage_conv[:].rearrange("p t o -> p (t o)"), conv_w).then_inc(conv_in, 16)
            sp.dma_start(stage_mask[:], block_mask).then_inc(conv_in, 16)
            sp.dma_start(stage_side[:], fside).then_inc(conv_in, 16)
            sp.dma_start(stage_ctx_w[:], ctx_w).then_inc(conv_in, 16)
            for n in range(RING, 2 * IC):
                load_slot(n)
            sp.dma_start(x_nat[:, TG:2 * TG, :], x_tile(x, 1)).then_inc(x_in[1], 16)
            for n in range(2 * IC, 3 * IC):
                load_slot(n)
            sp.wait_ge(q_ready, 3 * IC)
            for t in range(2, TILES):
                sp.dma_start(x_nat[:, t * TG:(t + 1) * TG, :], x_tile(x, t)).then_inc(x_in[t], 16)
            sp.wait_ge(down_mm, TILES * TG)
            sp.dma_start(ffn_f[:], ffn_w).then_inc(ffn_in, 16)
            for g in range(GROUPS):
                sp.wait_ge(o_ready, g + 1)
                sp.dma_start(out[g * P:(g + 1) * P, :], o_buf[:, g % 4, :]).then_inc(out_done[g % 4], 16)
            for n in range(4):
                sp.wait_ge(out_done[n], 16 * GROUPS // 4)

        @block.tensor
        def _(pe):
            mm = nc.tensor.matmul

            pe.wait_ge(cond_in, 16)
            mm(ps[:, 0, 0:B], w0_sb, cond_sb, start=True, stop=True).then_inc(h0_mm, 1)
            pe.wait_ge(h0_act, 1)
            mm(ps[:, 1, 0:B], w1_sb, h0[:], start=True, stop=True).then_inc(h1_mm, 1)
            pe.wait_ge(h1_act, 1)
            mm(ps[0:B, 2, 0:EXPERTS], h1[:], w2_sb, start=True, stop=True).then_inc(logit_mm, 1)
            pe.wait_ge(soft, 4)
            pe.wait_ge(lr_in, 3 * 16)
            nc.tensor.transpose(ps[0:EXPERTS, 3, 0:B], att[:], ident[0:B, 0:B]).then_inc(att_tr, 1)
            pe.wait_ge(att_ready, 1)
            pe.wait_ge(mixw_in, 2 * 16)
            for o in range(S // OB):
                last = mm(ps[:, 5, o * B:(o + 1) * B], cond_w_sb[:, o, :], att_t[:], start=True, stop=True)
            last.then_inc(mix_mm, 1)

            def mixed_bias(t):
                mm(ps[:, 4 + t, :], ones[0:EXPERTS, :],
                   att_bias[:].rearrange("k b s -> k (b s)")[:, t * TILE:(t + 1) * TILE],
                   start=True, stop=True).then_inc(aggb_mm, 1)

            pe.wait_ge(const_set, 1)
            pe.wait_ge(att_ready, 2)
            mixed_bias(0)

            def condition(t):
                pe.wait_ge(x_in[t], 16)
                for c in range(HC):
                    for g in range(t * TG, (t + 1) * TG):
                        last = mm(ps[:, c, (g % TG) * P:(g % TG + 1) * P], x_nat[:, g, c * P:(c + 1) * P],
                                  mix[:, g, :], start=True, stop=True)
                    last.then_inc(cond_mm, 1)
                    yield

            def down_low_rank_turn(t, j):
                n = t * TG + j
                pe.wait_ge(rep_ready, n + 1)
                nc.tensor.transpose(ps[:, 6 + j % 2, P:2 * P], t_rep[:, j % 2].rearrange("p m r -> p (m r)"),
                                    ident[:]).then_inc(rep_tr, 1)

            def down_low_rank(t, j):
                n = t * TG + j
                pe.wait_ge(t4d_hi_ready, n + 1)
                pe.wait_ge(t4d_lo_ready, n + 1)
                mm(ps[:, 6 + j % 2, :], t4d[:, j % 2, :], down_b4[:], start=True, stop=True).then_inc(down_l_mm, 1)

            def down(t, j):
                if j == 0:
                    pe.wait_ge(u_ready, t * IC + IC - 1)
                    if t == 0:
                        pe.wait_ge(down_ready, 1)
                if j >= 2:
                    pe.wait_ge(y_ready, t * TG + j - 1)
                for ic in range(IC):
                    k = width(ic)
                    if j == 0:
                        pe.wait_ge(h_lo_ready, t * IC + ic + 1)
                        if t == 0:
                            pe.wait_ge(q_ready, 2 * IC + ic + 1)
                    if j > 0 and ic == 3:
                        down_low_rank_turn(t, j - 1)
                    if j > 0 and ic == 8:
                        down_low_rank(t, j - 1)
                    for part in (h_hi, h_lo):
                        lhs = part[0:k, ic, j * P:(j + 1) * P]
                        first, end = ic == 0 and part is h_hi, ic == IC - 1 and part is h_lo
                        mm(ps[:, 4 + j % 2, :], lhs, down_w[0:k, ic, :], start=first, stop=end)
                        last = mm(ps[:, 6 + j % 2, 0:2 * R], lhs,
                                  down_a_w[0:k, ic].rearrange("p m r -> p (m r)"), start=first, stop=end)
                last.then_inc(down_mm, 1)

            def quantised(t, ic, m):
                if t == 0:
                    pe.wait_ge(q_ready, 2 * ic + m + 1)
                w = (gate_w, up_w)[m]
                k = width(ic)
                for c in range(HC):
                    for part in (x1_hi, x1_lo):
                        last = mm(ps[0:k, bank(ic, 2 * m), :], w[:, H * ic + c * k:H * ic + (c + 1) * k],
                                  part[:, c, :], start=c == 0 and part is x1_hi, stop=c == HC - 1 and part is x1_lo)
                last.then_inc(q_mm, 1)

            def low_rank(t, ic, m):
                w = (gate_b4, up_b4)[m]
                mm(ps[0:width(ic), bank(ic, 2 * m + 1), :], w[:, ic * P:ic * P + width(ic)], t4[m],
                   start=True, stop=True).then_inc(l_mm, 1)

            pe.wait_ge(mix_ready, 2)
            for _ in condition(0):
                pass
            pe.wait_ge(att_ready, 3)
            for t in range(1, TILES):
                mixed_bias(t)
            pe.wait_ge(conv_in, 4 * 16)
            pe.wait_ge(aggb_ready, 1)
            pair_cond = cond_sb.rearrange("p (n m) -> p n m", m=2)
            for q in range(4):
                last = mm(ps[q * S:(q + 1) * S, 4, 0:PAIRS], stage_ctx_w[:], pair_cond[:, :, q % 2],
                          start=True, stop=True)
            last.then_inc(ctx_mm, 1)
            pe.wait_ge(aggb_ready, TILES)
            pe.wait_ge(ctx_ready, 1)

            for t in range(TILES):
                if t == 0:
                    pe.wait_ge(lra_ready, 1)
                pe.wait_ge(x1_hi_ready, (t + 1) * HC)
                pe.wait_ge(x1_lo_ready, (t + 1) * HC)
                for c in range(HC):
                    for part in (x1_hi, x1_lo):
                        last = mm(ps[:, bank(0, 1), :], lr_a_w[:, c].rearrange("p m v r -> p (m v r)"),
                                  part[:, c, :], start=c == 0 and part is x1_hi,
                                  stop=c == HC - 1 and part is x1_lo)
                last.then_inc(p_mm, 1)
                if t > 0:
                    down_low_rank_turn(t - 1, TG - 1)
                quantised(t, 0, 0)
                if t > 0:
                    down_low_rank(t - 1, TG - 1)
                quantised(t, 0, 1)
                pe.wait_ge(p_hi_ready, t + 1)
                pe.wait_ge(p_lo_ready, t + 1)
                if t > 0:
                    pe.wait_ge(y_ready, t * TG)
                for m in range(2):
                    mm(ps[:, bank(1, 2 * m + 1), :], sel[:, m, :], p_hi, start=True, stop=False)
                    mm(ps[:, bank(1, 2 * m + 1), :], sel[:, m, :], p_lo, start=False, stop=True).then_inc(sel_mm, 1)
                quantised(t, 1, 0)
                quantised(t, 1, 1)
                if t == 0:
                    pe.wait_ge(lrb_ready, 2)
                for m in range(2):
                    pe.wait_ge(t4_hi_ready, 2 * t + m + 1)
                    pe.wait_ge(t4_lo_ready, 2 * t + m + 1)
                    low_rank(t, 0, m)
                low_rank(t, 1, 0)
                low_rank(t, 1, 1)
                for ic in range(2, IC):
                    pe.wait_ge(u_ready, t * IC + ic - 1)
                    for m in range(2):
                        quantised(t, ic, m)
                        low_rank(t, ic, m)
                down(t, 0)
                down(t, 1)
                down(t, 2)
                if t + 1 < TILES:
                    for _ in condition(t + 1):
                        pass
                down(t, 3)
            pe.wait_ge(conv_ready, 1)

            def turn(g):
                pe.wait_ge(z_ready, 2 * g + 2)
                if g >= 2:
                    pe.wait_ge(tt_ready, g - 1)
                for c in range(HC):
                    last = nc.tensor.transpose(ps[:, 4 + g % 2, c * P:(c + 1) * P],
                                               z_buf[:, g % 2, c * P:(c + 1) * P], ident[:])
                last.then_inc(z_tr, 1)

            def spread_scale(maxima, tr_sem, row_sem, mm_sem, col, row):
                pe.wait_ge(maxima, 1)
                nc.tensor.transpose(ps[0:1, 6, 0:P], amax[:, col:col + 1], ident[:]).then_inc(tr_sem, 1)
                pe.wait_ge(row_sem, 5)
                mm(ps[:, 7, 0:2], ones[0:1, :], small[0:1, row:row + 2], start=True, stop=True).then_inc(mm_sem, 1)

            for p in range(PAIRS):
                pe.wait_ge(stack_hi_ready, p + 1)
                pe.wait_ge(stack_lo_ready, p + 1)
                if p >= 4:
                    pe.wait_ge(z_ready, p - 3)
                for k in range(TAPS):
                    last = mm(ps[:, p % 4, :], conv_wt[:, k, :], stacked[p % STACKED][:, k:k + H],
                              start=k == 0, stop=k == TAPS - 1)
                last.then_inc(conv_mm, 1)
                if p == 0:
                    down_low_rank_turn(TILES - 1, TG - 1)
                if p == 1:
                    down_low_rank(TILES - 1, TG - 1)
                if p % 2 == 0 and p >= 2:
                    turn(p // 2 - 1)
                if p == 4:
                    spread_scale(wmax, wmax_tr, wmax, wsc_mm, GROUPS, 0)
            turn(GROUPS - 1)
            spread_scale(xmax, xmax_tr, xmax, xsc_mm, GROUPS + 1, 8)
            pe.wait_ge(ffn_ready, HC)
            for g in range(GROUPS):
                pe.wait_ge(q_fp8_ready, g + 1)
                if g >= 4:
                    pe.wait_ge(o_ready, g - 3)
                for c in range(HC):
                    last = mm(ps[:, g % 4, :], q_fp8[:, g % 2, c * P:(c + 1) * P], ffn_q[:, c * H:(c + 1) * H],
                              start=c == 0, stop=c == HC - 1)
                last.then_inc(ffn_mm, 1)

        @block.scalar
        def _(act):
            copy, activation = ACT.Copy, nc.scalar.activation
            act.wait_ge(cond_in, 16)
            act.wait_ge(h0_mm, 1)
            activation(h0[:], ps[:, 0, 0:B], ACT.Gelu, bias=b0_sb).then_inc(h0_act, 1)
            act.wait_ge(h1_mm, 1)
            activation(h1[:], ps[:, 1, 0:B], ACT.Gelu, bias=b1_sb).then_inc(h1_act, 1)
            act.wait_ge(soft, 2)
            activation(probs[:], logits[:], ACT.Exp, bias=stat[:, 0:1], accum_out=stat[:, 1:2]).then_inc(exp_done, 1)
            act.wait_ge(lr_in, 3 * 16)
            activation(sel[:], stage_sel[:], copy)
            activation(lr_a_w[:, :, :, 0, :], stage_lr_a[:], copy).then_inc(lra_hi, 1)
            act.wait_ge(mix_mm, 1)
            act.wait_ge(mix_zero, 1)
            for q in range(2, OB):
                last = spread_mix(activation, q, (copy,))
            last.then_inc(mix_ready, 1)
            def split_mixed(t):
                for c in range(HC):
                    act.wait_ge(xs_ready, t * HC + c + 1)
                    activation(x1_hi[:, c, :], split_buf[c], copy).then_inc(x1_hi_ready, 1)

            def keep_bias(t):
                act.wait_ge(aggb_mm, t + 1)
                activation(agg_b[:, t * TILE:(t + 1) * TILE], ps[:, 4 + t, :], copy).then_inc(aggb_ready, 1)

            keep_bias(0)
            act.wait_ge(lrb_in, 2 * 16)
            activation(gate_b4[:], stage_gate_b[:], copy).then_inc(lrb_hi, 1)
            activation(up_b4[:], stage_up_b[:], copy).then_inc(lrb_hi, 1)
            split_mixed(0)
            for t in range(1, TILES):
                keep_bias(t)
            act.wait_ge(down_in, 3 * 16)
            activation(down_a_w[:, :, 0, :], stage_down_a[:], copy).then_inc(down_hi, 1)
            activation(down_b4[:], stage_down_b[:], copy).then_inc(down_hi, 1)
            act.wait_ge(conv_full, 1)
            activation(conv_wt[:, :, 0:64], y_buf[:].rearrange("p a b -> p (a b)")[:, 0:TAPS * 64]
                       .rearrange("p (t o) -> p t o", t=TAPS), copy).then_inc(conv_hi, 1)

            def down_part(t, j):
                act.wait_ge(down_mm, t * TG + j + 1)
                activation(t_part[:, j % 2, :], ps[:, 6 + j % 2, R:2 * R], copy,
                           scale=LR_SCALE).then_inc(part_ready, 1)

            def down_t4(t, j):
                act.wait_ge(rep_tr, t * TG + j + 1)
                activation(t4d[:, j % 2, :], ps[:, 6 + j % 2, P:2 * P], copy).then_inc(t4d_hi_ready, 1)

            def h_high(t, ic):
                n = t * IC + ic
                act.wait_ge(h_ready, n + 1)
                k = width(ic)
                activation(h_hi[0:k, ic, :], a_buf[0:k, ic % 2, :], copy).then_inc(h_hi_ready, 1)

            def stack_high(p):
                r0, g = 64 * (p % 2), p // 2
                act.wait_ge(x2_ready, g + 1)
                if p >= STACKED:
                    act.wait_ge(conv_mm, p - STACKED + 1)
                activation(stacked[p % STACKED][r0:r0 + 64, PAD:PAD + H], x_nat[r0:r0 + 64, g, :],
                           copy).then_inc(stack_hi_ready, 1)

            for t in range(TILES):
                act.wait_ge(p_mm, t + 1)
                activation(p_hi, ps[:, bank(0, 1), :], copy, scale=LR_SCALE).then_inc(p_hi_ready, 1)
                if t > 0:
                    down_t4(t - 1, TG - 1)
                if t == 0:
                    act.wait_ge(scale_ready, 2)
                for ic in range(IC):
                    n = t * IC + ic
                    k = width(ic)
                    act.wait_ge(q_mm, 2 * n + 1)
                    if ic >= 2:
                        act.wait_ge(h_lo_ready, n - 1)
                    activation(a_buf[0:k, ic % 2, :], ps[0:k, bank(ic, 0), :], copy,
                               scale=gate_sc[0:k, ic:ic + 1]).then_inc(ag_ready, 1)
                    act.wait_ge(q_mm, 2 * n + 2)
                    activation(b_buf[0:k, ic % 2, :], ps[0:k, bank(ic, 2), :], copy,
                               scale=up_sc[0:k, ic:ic + 1]).then_inc(au_ready, 1)
                    if ic == 0:
                        for m in range(2):
                            act.wait_ge(sel_mm, 2 * t + m + 1)
                            activation(t4[m], ps[:, bank(1, 2 * m + 1), :], copy).then_inc(t4_hi_ready, 1)
                    if ic >= 1:
                        h_high(t, ic - 1)
                    act.wait_ge(g_ready, n + 1)
                    activation(a_buf[0:k, ic % 2, :], a_buf[0:k, ic % 2, :], ACT.Silu).then_inc(silu_ready, 1)
                h_high(t, IC - 1)
                for j in range(TG):
                    down_part(t, j)
                    if j == 2 and t + 1 < TILES:
                        split_mixed(t + 1)
                    if j < TG - 1:
                        down_t4(t, j)
                    if t == TILES - 1 and j == 0:
                        for p in range(STACKED):
                            stack_high(p)

            def keep_turned(g):
                act.wait_ge(z_tr, g + 1)
                activation(t_t[:, :, g * P:(g + 1) * P], ps[:, 4 + g % 2, :].rearrange("p (c q) -> p c q", c=HC),
                           copy).then_inc(tt_ready, 1)

            for p in range(PAIRS):
                if 1 <= p < PAIRS - STACKED + 1:
                    stack_high(p + STACKED - 1)
                if p == 1:
                    down_t4(TILES - 1, TG - 1)
                act.wait_ge(conv_mm, p + 1)
                if p >= 2:
                    act.wait_ge(z_ready, p - 1)
                activation(conv_part[:, p % 2, :], ps[64:P, p % 4, :], ACT.Identity,
                           bias=ctx_bias[64:P, p:p + 1]).then_inc(part_out, 1)
                if p % 2 == 1 and p >= 3:
                    keep_turned(p // 2 - 1)
            keep_turned(GROUPS - 1)
            act.wait_ge(scales_ready, 3)
            for g in range(GROUPS):
                if g >= 2:
                    act.wait_ge(exp_ready, g - 1)
                activation(v16[:, g % 2, :].rearrange("p (c q) -> p c q", c=HC), t_t[:, :, g * P:(g + 1) * P], copy,
                           scale=small[:, 16:17]).then_inc(v_ready, 1)

        @block.gpsimd
        def _(pool):
            nc.gpsimd.memset(mix[:], 0.0).then_inc(mix_zero, 1)
            for m, (w, st) in enumerate(((gate_b4, stage_gate_b), (up_b4, stage_up_b))):
                pool.wait_ge(lrb_hi, m + 1)
                for q in (1, 3):
                    rows = slice(q * S, (q + 1) * S)
                    last = nc.gpsimd.tensor_tensor(w[rows, :], st[rows, :], plain(w[rows, :]), ALU.subtract)
                last.then_inc(lrb_ready, 1)
            for t in range(TILES):
                for ic in range(IC):
                    n = t * IC + ic
                    k = width(ic)
                    pool.wait_ge(h_hi_ready, n + 1)
                    nc.gpsimd.tensor_tensor(h_lo[0:k, ic, :], a_buf[0:k, ic % 2, :], plain(h_hi[0:k, ic, :]),
                                            ALU.subtract).then_inc(h_lo_ready, 1)
                    if ic == 1 and t > 0:
                        n = t * TG - 1
                        pool.wait_ge(y_ready, n + 1)
                        nc.gpsimd.tensor_tensor(x_nat[:, n, :], y_buf[:, n % 2, :], x_nat[:, n, :],
                                                ALU.add).then_inc(x2_ready, 1)
                for j in range(TG - 1 if t + 1 < TILES else TG):
                    n = t * TG + j
                    pool.wait_ge(y_ready, n + 1)
                    nc.gpsimd.tensor_tensor(x_nat[:, n, :], y_buf[:, j % 2, :], x_nat[:, n, :],
                                            ALU.add).then_inc(x2_ready, 1)
            for g in range(GROUPS):
                pool.wait_ge(v_plus_ready, g + 1)
                if g >= 2:
                    pool.wait_ge(q_fp8_ready, g - 1)
                nc.gpsimd.tensor_tensor(q_raw[:, g % 2, :], v_plus[:, g % 2, :], m16[:, g % 2, :],
                                        ALU.subtract).then_inc(q_raw_ready, 1)

        @block.vector
        def _(dve):
            v = nc.vector
            v.memset(ones[:], 1.0).then_inc(const_set, 1)
            dve.wait_ge(cond_in, 16)
            dve.wait_ge(logit_mm, 1)
            v.tensor_tensor(logits[:], ps[0:B, 2, 0:EXPERTS], b2_sb, ALU.add).then_inc(soft, 1)
            dve.wait_ge(soft, 1)
            v.tensor_reduce(stat[:, 0:1], logits[:], AX_X, ALU.max, negate=True).then_inc(soft, 1)
            dve.wait_ge(exp_done, 1)
            v.reciprocal(stat[:, 2:3], stat[:, 1:2]).then_inc(soft, 1)
            dve.wait_ge(soft, 3)
            v.tensor_scalar(att[:], probs[:], stat[:, 2:3], None, ALU.mult).then_inc(soft, 1)
            dve.wait_ge(att_tr, 1)
            v.tensor_copy(att_t[:], ps[0:EXPERTS, 3, 0:B]).then_inc(att_ready, 1)
            dve.wait_ge(att_ready, 1)
            dve.wait_ge(mixw_in, 2 * 16)

            def expert_bias(b0, b1):
                v.tensor_tensor(att_bias[:, b0:b1], att_t[:, b0:b1].unsqueeze(2).to_broadcast([EXPERTS, b1 - b0, S]),
                                bias_k_sb[:].unsqueeze(1).to_broadcast([EXPERTS, b1 - b0, S]),
                                ALU.mult).then_inc(att_ready, 1)

            expert_bias(0, TILE // S)
            dve.wait_ge(mix_mm, 1)
            dve.wait_ge(mix_zero, 1)
            for q in range(2):
                last = spread_mix(v.tensor_copy, q, ())
            last.then_inc(mix_ready, 1)
            expert_bias(TILE // S, B)

            def convert(n):
                dve.wait_ge(q_in[n % RING], 16 * (n // RING + 1))
                v.tensor_scalar(slot_weights(n), slot(n), Q_ZERO, None, ALU.subtract).then_inc(q_ready, 1)

            def split_mixed(t):
                for c in range(HC):
                    dve.wait_ge(cond_mm, t * HC + c + 1)
                    v.tensor_tensor(split_buf[c], ps[:, c, :], agg_b[:, t * TILE:(t + 1) * TILE],
                                    ALU.add).then_inc(xs_ready, 1)
                    if c > 0:
                        split_low(t, c - 1)
                split_low(t, HC - 1)

            def split_low(t, c):
                dve.wait_ge(x1_hi_ready, t * HC + c + 1)
                v.tensor_tensor(x1_lo[:, c, :], split_buf[c], plain(x1_hi[:, c, :]),
                                ALU.subtract).then_inc(x1_lo_ready, 1)

            dve.wait_ge(lra_hi, 1)
            v.tensor_tensor(lr_a_w[:, :, :, 1, :], stage_lr_a[:], plain(lr_a_w[:, :, :, 0, :]),
                            ALU.subtract).then_inc(lra_ready, 1)
            convert(0)
            convert(1)
            dve.wait_ge(aggb_ready, 1)
            split_mixed(0)
            dve.wait_ge(scale_in, 2 * 16)
            v.tensor_scalar(gate_sc[:], gate_sc[:], Q_STEP, None, ALU.mult).then_inc(scale_ready, 1)
            v.tensor_scalar(up_sc[:], up_sc[:], Q_STEP, None, ALU.mult).then_inc(scale_ready, 1)
            dve.wait_ge(conv_in, 4 * 16)
            dve.wait_ge(ctx_mm, 1)
            v.tensor_scalar(ctx_bias[:], ps[:, 4, 0:PAIRS], stage_side[:], None, ALU.add).then_inc(ctx_ready, 1)
            convert(2)
            convert(3)
            dve.wait_ge(down_hi, 2)
            v.tensor_tensor(down_a_w[:, :, 1, :], stage_down_a[:], plain(down_a_w[:, :, 0, :]), ALU.subtract)
            for q in (1, 3):
                rows = slice(q * S, (q + 1) * S)
                v.tensor_tensor(down_b4[rows, :], stage_down_b[rows, :], plain(down_b4[rows, :]), ALU.subtract)
            dve.wait_ge(down_in, 3 * 16)
            v.tensor_scalar(down_sb[:], down_sb[:], Q_STEP, None, ALU.mult).then_inc(down_ready, 1)
            full = y_buf[:].rearrange("p a b -> p (a b)")[:, 0:TAPS * 64]
            v.tensor_tensor(full.rearrange("p (t n o) -> p t n o", t=TAPS, o=CG),
                            stage_conv[:].unsqueeze(2).to_broadcast([P, TAPS, 2 * CONV_GROUPS, CG]),
                            stage_mask[:].unsqueeze(1).unsqueeze(3).to_broadcast([P, TAPS, 2 * CONV_GROUPS, CG]),
                            ALU.mult).then_inc(conv_full, 1)
            dve.wait_ge(conv_hi, 1)
            v.tensor_tensor(conv_wt[:, :, 64:P], full.rearrange("p (t o) -> p t o", t=TAPS),
                            plain(conv_wt[:, :, 0:64]), ALU.subtract).then_inc(conv_ready, 1)

            def down_rep(t, j):
                n = t * TG + j
                dve.wait_ge(part_ready, n + 1)
                v.scalar_tensor_tensor(t_rep[:, j % 2], ps[:, 6 + j % 2, 0:R].unsqueeze(1).to_broadcast([P, 4, R]),
                                       LR_SCALE, t_part[:, j % 2].unsqueeze(1).to_broadcast([P, 4, R]),
                                       ALU.mult, ALU.add).then_inc(rep_ready, 1)

            def down_scaled(t, j):
                n = t * TG + j
                if n >= 2:
                    dve.wait_ge(x2_ready, n - 1)
                v.tensor_tensor(y_buf[:, j % 2, :], ps[:, 4 + j % 2, :], down_sb[:], ALU.mult).then_inc(yq_ready, 1)

            def down_t4(t, j):
                dve.wait_ge(t4d_hi_ready, t * TG + j + 1)
                v.tensor_tensor(t4d[64:P, j % 2, :], ps[64:P, 6 + j % 2, P:2 * P], plain(t4d[64:P, j % 2, :]),
                                ALU.subtract).then_inc(t4d_lo_ready, 1)

            def down_sum(t, j):
                n = t * TG + j
                dve.wait_ge(down_l_mm, n + 1)
                dve.wait_ge(yq_ready, n + 1)
                v.tensor_tensor(y_buf[:, j % 2, :], ps[:, 6 + j % 2, :], y_buf[:, j % 2, :],
                                ALU.add).then_inc(y_ready, 1)

            def stack_low(p):
                r0, g = 64 * (p % 2), p // 2
                dve.wait_ge(stack_hi_ready, p + 1)
                s = stacked[p % STACKED]
                v.tensor_tensor(s[64 - r0:P - r0, PAD:PAD + H], x_nat[r0:r0 + 64, g, :],
                                plain(s[r0:r0 + 64, PAD:PAD + H]), ALU.subtract).then_inc(stack_lo_ready, 1)

            for t in range(TILES):
                if t > 0:
                    down_t4(t - 1, TG - 1)
                dve.wait_ge(p_hi_ready, t + 1)
                v.scalar_tensor_tensor(p_lo, ps[:, bank(0, 1), :], LR_SCALE, plain(p_hi), ALU.mult,
                                       ALU.subtract).then_inc(p_lo_ready, 1)
                if t > 0:
                    down_sum(t - 1, TG - 1)
                for m in range(2):
                    dve.wait_ge(t4_hi_ready, 2 * t + m + 1)
                    v.tensor_tensor(t4[m][64:P], ps[64:P, bank(1, 2 * m + 1), :], plain(t4[m][64:P]),
                                    ALU.subtract).then_inc(t4_lo_ready, 1)
                for ic in range(IC):
                    n = t * IC + ic
                    k = width(ic)
                    a, b = a_buf[0:k, ic % 2, :], b_buf[0:k, ic % 2, :]
                    if t == 0:
                        for later in range(2 * ic + 4, min(2 * ic + 6, 2 * IC)):
                            convert(later)
                        if 2 * ic + 4 >= 2 * IC:
                            for later in range(2 * IC + 2 * (ic - IC + 2), 2 * IC + 2 * (ic - IC + 3)):
                                convert(later)
                    dve.wait_ge(ag_ready, n + 1)
                    dve.wait_ge(l_mm, 2 * n + 1)
                    v.tensor_tensor(a, ps[0:k, bank(ic, 1), :], a, ALU.add).then_inc(g_ready, 1)
                    dve.wait_ge(au_ready, n + 1)
                    dve.wait_ge(l_mm, 2 * n + 2)
                    v.tensor_tensor(b, ps[0:k, bank(ic, 3), :], b, ALU.add).then_inc(u_ready, 1)
                    dve.wait_ge(silu_ready, n + 1)
                    dve.wait_ge(u_ready, n + 1)
                    v.tensor_tensor(a, a, b, ALU.mult).then_inc(h_ready, 1)
                if t == 0:
                    for later in range(2 * IC + 4, 3 * IC):
                        convert(later)
                for j in range(TG):
                    down_rep(t, j)
                    down_scaled(t, j)
                    if j < TG - 1:
                        if j == 2 and t + 1 < TILES:
                            split_mixed(t + 1)
                        down_t4(t, j)
                        down_sum(t, j)
                    if t == TILES - 1 and j == 0:
                        for s in stacked:
                            v.memset(plain(s[:, 0:PAD]), 0.0)
                            v.memset(plain(s[:, PAD + H:]), 0.0)
                        for p in range(STACKED):
                            stack_low(p)

            def scale_from(maxima, tr_sem, row):
                dve.wait_ge(tr_sem, 1)
                largest = small[0:1, row + 2:row + 3]
                v.tensor_reduce(largest, ps[0:1, 6, 0:P], AX_X, ALU.max).then_inc(maxima, 1)
                dve.wait_ge(maxima, 2)
                v.tensor_scalar(largest, largest, AMAX_MIN, None, ALU.max).then_inc(maxima, 1)
                dve.wait_ge(maxima, 3)
                v.reciprocal(small[0:1, row:row + 1], largest).then_inc(maxima, 1)
                v.tensor_scalar(small[0:1, row + 1:row + 2], largest, 1.0 / FP8_MAX, None,
                                ALU.mult).then_inc(maxima, 1)

            weight_steps = [0]

            def step(ins):
                ins.then_inc(wq_step, 1)
                weight_steps[0] += 1
                dve.wait_ge(wq_step, weight_steps[0])

            for p in range(PAIRS):
                if 1 <= p < PAIRS - STACKED + 1:
                    stack_low(p + STACKED - 1)
                if p == 1:
                    down_t4(TILES - 1, TG - 1)
                r0, g = 64 * (p % 2), p // 2
                dve.wait_ge(part_out, p + 1)
                if g >= 2 and p % 2 == 0:
                    dve.wait_ge(z_tr, g - 1)
                v.tensor_tensor(z_buf[r0:r0 + 64, g % 2, :], ps[0:64, p % 4, :], conv_part[:, p % 2, :],
                                ALU.add).then_inc(z_ready, 1)
                if p == 1:
                    down_sum(TILES - 1, TG - 1)
                if p % 2 == 1:
                    dve.wait_ge(z_ready, p + 1)
                    v.tensor_reduce(amax[:, g:g + 1], z_buf[:, g % 2, :], AX_X, ALU.max,
                                    apply_absolute_value=True).then_inc(amax_ready, 1)
                if p == 2:
                    dve.wait_ge(ffn_in, 16)
                    v.tensor_reduce(amax[:, GROUPS:GROUPS + 1], ffn_f[:], AX_X, ALU.max,
                                    apply_absolute_value=True).then_inc(wmax, 1)
                if p == 4:
                    scale_from(wmax, wmax_tr, 0)
                if p == 6:
                    dve.wait_ge(wsc_mm, 1)
                    v.tensor_scalar(small[:, 18:19], ps[:, 7, 0:1], FP8_MAX, None, ALU.mult).then_inc(scales_ready, 1)
                    v.tensor_copy(small[:, 19:20], ps[:, 7, 1:2]).then_inc(scales_ready, 1)
                    dve.wait_ge(scales_ready, 2)
                if 8 <= p < 8 + 2 * HC and p % 2 == 0:
                    c = (p - 8) // 2
                    w = ffn_f[:, c * H:(c + 1) * H]
                    step(v.tensor_scalar(v16[:, 0, :], w, small[:, 18:19], None, ALU.mult))
                    step(v.tensor_scalar(e16[:, 0, :].bitcast(U16), v16[:, 0, :].bitcast(U16), EXP_MASK, None,
                                         ALU.bitwise_and))
                    step(v.tensor_scalar(m16[:, 0, :], e16[:, 0, :], E4M3_MIN_NORMAL, ROUND_AT_3_BITS,
                                         ALU.max, ALU.mult))
                    step(v.scalar_tensor_tensor(v_plus[:, 0, :], w, small[:, 18:19], m16[:, 0, :],
                                                ALU.mult, ALU.add))
                    step(v.tensor_tensor(q_raw[:, 0, :], v_plus[:, 0, :], m16[:, 0, :], ALU.subtract))
                    v.tensor_scalar(ffn_q[:, c * H:(c + 1) * H], q_raw[:, 0, :], FP8_MAX, -FP8_MAX,
                                    ALU.min, ALU.max).then_inc(ffn_ready, 1)
            dve.wait_ge(amax_ready, GROUPS)
            v.tensor_reduce(amax[:, GROUPS + 1:GROUPS + 2], amax[:, 0:GROUPS], AX_X, ALU.max).then_inc(xmax, 1)
            scale_from(xmax, xmax_tr, 8)
            dve.wait_ge(xsc_mm, 1)
            v.tensor_scalar(small[:, 16:17], ps[:, 7, 0:1], FP8_MAX, None, ALU.mult).then_inc(scales_ready, 1)
            v.tensor_scalar(small[:, 17:18], ps[:, 7, 1:2], small[:, 19:20], None, ALU.mult).then_inc(scales_ready, 1)
            dve.wait_ge(scales_ready, 4)

            def clip(g):
                dve.wait_ge(q_raw_ready, g + 1)
                if g >= 2:
                    dve.wait_ge(ffn_mm, g - 1)
                v.tensor_scalar(q_fp8[:, g % 2, :], q_raw[:, g % 2, :], FP8_MAX, -FP8_MAX,
                                ALU.min, ALU.max).then_inc(q_fp8_ready, 1)

            def output(g):
                dve.wait_ge(ffn_mm, g + 1)
                if g >= 4:
                    dve.wait_ge(out_done[g % 4], 16 * (g // 4))
                v.scalar_tensor_tensor(o_buf[:, g % 4, :], ps[:, g % 4, :], small[:, 17:18], x_nat[:, g, :],
                                       ALU.mult, ALU.add).then_inc(o_ready, 1)

            for g in range(GROUPS):
                e, m = e16[:, g % 2, :], m16[:, g % 2, :]
                dve.wait_ge(v_ready, g + 1)
                v.tensor_scalar(e.bitcast(U16), v16[:, g % 2, :].bitcast(U16), EXP_MASK, None,
                                ALU.bitwise_and).then_inc(exp_ready, 1)
                if g >= 2:
                    dve.wait_ge(q_raw_ready, g - 1)
                dve.wait_ge(exp_ready, g + 1)
                v.tensor_scalar(m, e, E4M3_MIN_NORMAL, ROUND_AT_3_BITS, ALU.max, ALU.mult).then_inc(m_ready, 1)
                dve.wait_ge(m_ready, g + 1)
                v.scalar_tensor_tensor(v_plus[:, g % 2, :].rearrange("p (c q) -> p c q", c=HC),
                                       t_t[:, :, g * P:(g + 1) * P], small[:, 16:17],
                                       m.rearrange("p (c q) -> p c q", c=HC), ALU.mult,
                                       ALU.add).then_inc(v_plus_ready, 1)
                if g >= 1:
                    clip(g - 1)
                if g >= 2:
                    output(g - 2)
            clip(GROUPS - 1)
            output(GROUPS - 2)
            output(GROUPS - 1)


def kernel(x, cond_128, fside_S_0, L0_cond_W0, L0_cond_b0, L0_cond_W1, L0_cond_b1, L0_cond_W2, L0_cond_b2,
           L0_cond_weight, L0_cond_bias_k, L0_ffn_gate_q, L0_ffn_gate_scale, L0_ffn_gate_A, L0_ffn_gate_B,
           L0_ffn_up_q, L0_ffn_up_scale, L0_ffn_up_A, L0_ffn_up_B, L0_ffn_down_q, L0_ffn_down_scale,
           L0_ffn_down_A, L0_ffn_down_B, L1_cond_weight, L1_cond_c_weight, L1_ffn_weight):
    import numpy as np
    import concourse.bacc as bacc
    from concourse.bass_utils import run_bass_kernel_spmd

    a = np.asarray

    def chunked(w):
        w = a(w).T.reshape(HC, P, I)
        return np.concatenate([w[:, :, ic * P:ic * P + width(ic)].transpose(1, 0, 2).reshape(P, -1)
                               for ic in range(IC)], axis=1)

    def by_chunk(w):
        w = a(w)
        w = np.concatenate([w, np.zeros((IC * P - I,) + w.shape[1:], w.dtype)])
        return w.reshape(IC, P, -1).transpose(1, 0, 2).reshape(P, -1)

    def broadcast(w, n):
        return np.broadcast_to(a(w)[None, :], (n, len(w)))

    lr_a = np.stack([a(L0_ffn_gate_A), a(L0_ffn_up_A)], axis=1).reshape(HC, P, 2 * R).transpose(1, 0, 2)
    cond_pack = np.zeros((P, COND_COLS), np.float32)
    for at, w in zip(COND_AT, (a(cond_128).T, a(L0_cond_W0), a(L0_cond_W1), a(L0_cond_W2), a(L0_cond_b0)[:, None],
                               a(L0_cond_b1)[:, None], broadcast(L0_cond_b2, B))):
        cond_pack[:w.shape[0], at:at + w.shape[1]] = w
    conv_w = a(L1_cond_weight).reshape(CONV_GROUPS, CG, CG, TAPS).transpose(0, 2, 3, 1).reshape(S, TAPS * CG)
    row, col = np.arange(P)[:, None], np.arange(2 * CONV_GROUPS)[None, :]
    block_mask = ((row // S % 2 == col // CONV_GROUPS) & (row % S // CG == col % CONV_GROUPS)).astype(np.float32)
    row, col = np.arange(P)[:, None], np.arange(2 * P)[None, :]
    sel = ((row % R == col % R) & (row // (2 * R) == col // P)).astype(np.float32)
    arrays = {
        "x": a(x).reshape(TOKENS, H), "cond_pack": cond_pack,
        "cond_w": a(L0_cond_weight).reshape(EXPERTS, S * S), "bias_k": a(L0_cond_bias_k),
        "gate_q": chunked(L0_ffn_gate_q), "up_q": chunked(L0_ffn_up_q),
        "gate_s": by_chunk(L0_ffn_gate_scale), "up_s": by_chunk(L0_ffn_up_scale),
        "lr_a": lr_a.reshape(P, -1), "gate_b": np.tile(a(L0_ffn_gate_B), (4, 1)),
        "up_b": np.tile(a(L0_ffn_up_B), (4, 1)),
        "down_q": by_chunk(a(L0_ffn_down_q).T), "down_s": broadcast(L0_ffn_down_scale, P),
        "down_a": by_chunk(L0_ffn_down_A), "down_b": np.tile(a(L0_ffn_down_B), (4, 1)),
        "conv_w": np.tile(conv_w, (4, 1)), "ctx_w": a(L1_cond_c_weight).T,
        "fside": np.tile(a(fside_S_0), 4)[:, None],
        "ffn_w": a(L1_ffn_weight).reshape(HC, P, H).transpose(1, 0, 2).reshape(P, -1),
        "block_mask": block_mask, "ident": np.eye(P, dtype=np.float32), "sel": sel,
    }
    arrays = {f"in_{k}": np.ascontiguousarray(v) for k, v in arrays.items()}
    nc = bacc.Bacc("TRN2", target_bir_lowering=False, num_devices=1, dynamic_dma_scratch_size=1024)
    aps = [nc.dram_tensor(k, v.shape, mybir.dt.from_np(v.dtype), kind="ExternalInput").ap()
           for k, v in arrays.items()]
    out = nc.dram_tensor("out", (TOKENS, H), F32, kind="ExternalOutput").ap()
    build(nc, *aps, out)
    r = run_bass_kernel_spmd(nc, [arrays], core_ids=[0])
    return r.results[0]["out"].reshape(B, S, H)
```

```python
from contextlib import ExitStack

import concourse.bass as bass
from concourse import mybir

F32 = mybir.dt.float32
F32R = mybir.dt.float32r
BF16 = mybir.dt.bfloat16
I32 = mybir.dt.int32
ACT = mybir.ActivationFunctionType
ALU = mybir.AluOpType
AX_X = mybir.AxisListType.X

P = 128
B, S, H = 64, 32, 512
TOKENS = B * S
I = 1376
R = 32
EXPERTS = 8
TAPS, PAD = 9, 4
CONV_GROUPS = 4
Q_ZERO, Q_STEP, LR_SCALE = 7.5, 0.005, 0.02
FP8_MAX, AMAX_MIN = 448.0, 1e-12

HC = H // P
IC = -(-I // P)
GROUPS = TOKENS // P
GB = P // S
TILE = 512
TILES = TOKENS // TILE
TG = TILE // P
PHASES = H // P
SHIFTS = 3
Q = 2 * GB
CG = S // CONV_GROUPS
STEPS = (1,) + (2,) * (GROUPS // 2 - 1) + (1,)
RING = 8
WARM = (5, 4, 1, 7)
BIAS_BANK = (4, 5, 7, 6)
XT = 4
CONV_AFTER = (3, 3, 2, 8)
CONV_FROM = tuple(sum(CONV_AFTER[:j]) for j in range(TG))
XMAX, WMAX = PHASES * GROUPS, PHASES * GROUPS + 2
W_SPREAD = 5
W_STEPS = 4
ROUND_SCALE, ROUND_MIN = 2.0 ** 20, 1.5 * 2.0 ** 14
COND_WIDTHS = (B, P, P, EXPERTS, 1, 1, EXPERTS)
COND_AT = tuple(sum(COND_WIDTHS[:n]) for n in range(len(COND_WIDTHS)))
COND_COLS = sum(COND_WIDTHS)
OB = P // S


def width(ic):
    return min(P, I - ic * P)


def build(nc, x, cond_pack, cond_w, bias_k, gate_q, up_q, gate_s, up_s,
          lr_a, gate_b, up_b, down_q, down_s, down_a, down_b, conv_w, ctx_w, fside, ffn_w,
          batch_mask, ident_in, sel_in, turned, out):
    with ExitStack() as ctx:
        def sb(name, shape, dt, stack=ctx):
            return stack.enter_context(nc.sbuf_tensor(name, shape, dt))

        def sem(name):
            return ctx.enter_context(nc.semaphore(name))

        ps = ctx.enter_context(nc.psum_tensor("ps", [P, 8, 512], F32))

        x_nat = sb("x_nat", [P, GROUPS, H], F32)
        conv_wt = sb("conv_wt", [P, SHIFTS, 2, P], F32R)
        ctx_rhs = sb("ctx_rhs", [B, GB, 2, S], F32R)
        ctx_pick = sb("ctx_pick", [B, GROUPS], F32R)
        stage = sb("stage", [P, 2, H], F32R)
        diag = sb("diag", [P, P], F32)
        ident = sb("ident", [P, P], F32)
        ones = sb("ones", [P, P], F32)
        y_buf = sb("y_buf", [P, 2, H], F32)
        small = sb("small", [P, 64], F32)
        amax = sb("amax", [P, WMAX + HC], F32)
        x1_hi = sb("x1_hi", [P, HC, TILE], F32R)
        x1_lo = sb("x1_lo", [P, HC, TILE], F32R)
        down_w = sb("down_w", [P, IC, H], F32R)
        gate_b4 = sb("gate_b4", [P, I], F32R)
        up_b4 = sb("up_b4", [P, I], F32R)
        down_b4 = sb("down_b4", [P, H], F32R)
        lr_a_w = sb("lr_a_w", [P, HC, 2, 2, R], F32R)
        down_a_w = sb("down_a_w", [P, IC, 2, R], F32R)
        down_sb = sb("down_sb", [P, H], F32)
        agg_b = sb("agg_b", [P, TOKENS], F32)
        mix = sb("mix", [P, GROUPS, P], F32)
        a_buf = sb("a_buf", [P, 2, TILE], F32)
        b_buf = sb("b_buf", [P, 2, TILE], F32)
        sel = sb("sel", [P, 2, P], F32R)
        gate_sc = sb("gate_sc", [P, IC], F32)
        up_sc = sb("up_sc", [P, IC], F32)
        pd_hi = sb("pd_hi", [2 * R, TILE], F32R)
        pd_lo = sb("pd_lo", [2 * R, TILE], F32R)
        t4d = sb("t4d", [P, TILE], F32R)
        phase1 = ExitStack()
        gate_w = sb("gate_w", [P, HC * I], F32R, phase1)
        up_w = sb("up_w", [P, HC * I], F32R, phase1)
        h_hi = sb("h_hi", [P, IC, TILE], F32R, phase1)
        h_lo = sb("h_lo", [P, IC, TILE], F32R, phase1)
        phase1.close()
        early = ExitStack()
        pad_gate = sb("pad_gate", [P, 2 * HC * I], F32, early)
        cond_in_sb = sb("cond_in_sb", [P, COND_COLS], F32, early)
        h0 = sb("h0", [P, B], F32, early)
        h1 = sb("h1", [P, B], F32, early)
        logits = sb("logits", [B, EXPERTS], F32, early)
        probs = sb("probs", [B, EXPERTS], F32, early)
        att = sb("att", [B, EXPERTS], F32, early)
        att_t = sb("att_t", [EXPERTS, B], F32, early)
        stat = sb("stat", [B, 4], F32, early)
        bias_k_sb = sb("bias_k_sb", [EXPERTS, S], F32, early)
        cond_w_sb = sb("cond_w_sb", [EXPERTS, S // OB, P], F32, early)
        att_bias = sb("att_bias", [EXPERTS, B, S], F32, early)
        stage_lr_a = sb("stage_lr_a", [P, HC, 2, R], F32, early)
        stage_sel = sb("stage_sel", [P, 2, P], F32, early)
        stage_mask = sb("stage_mask", [B, GB + GROUPS], F32, early)
        stage_side = sb("stage_side", [B, S], F32, early)
        stage_ctx_w = sb("stage_ctx_w", [P, S], F32, early)
        used = 4 * (COND_COLS + 2 * B + 3 * EXPERTS + B + 4 + S + S // OB * P + B * S + HC * 2 * R + 2 * P
                    + GB + GROUPS + S + S)
        pad_h = sb("pad_h", [P, (4 * IC * TILE - used) // 4 + 32], F32, early)
        stage_gate_b = sb("stage_gate_b", [P, I], F32, early)
        stage_up_b = sb("stage_up_b", [P, I], F32, early)
        stage_down_b = sb("stage_down_b", [P, H], F32, early)
        stage_down_a = sb("stage_down_a", [P, IC, R], F32, early)
        stage_conv = sb("stage_conv", [P, SHIFTS, P], F32, early)
        early.close()
        cond_sb, w0_sb, w1_sb, w2_sb, b0_sb, b1_sb, b2_sb = (
            cond_in_sb[0:rows, COND_AT[n]:COND_AT[n] + COND_WIDTHS[n]]
            for n, rows in enumerate((P, P, P, P, P, P, B)))
        phase2 = ExitStack()
        t_t = sb("t_t", [P, HC, TOKENS], F32, phase2)
        xt_own = [sb(f"xt{n}", [P, Q, P + 2], F32R, phase2) for n in range(2)]
        pad_2 = sb("pad_2", [P, 2 * HC * I - HC * TOKENS - 2 * Q * (P + 2)], F32, phase2)
        v16 = sb("v16", [P, 2, 2 * H], BF16, phase2)
        m16 = sb("m16", [P, 2, 2 * H], BF16, phase2)
        v_plus = sb("v_plus", [P, 2, 2 * H], F32, phase2)
        q_raw = sb("q_raw", [P, 2, 2 * H], BF16, phase2)
        q_fp8 = sb("q_fp8", [P, 2, 2 * H], BF16, phase2)
        o_buf = sb("o_buf", [P, 2, 2 * H], F32, phase2)
        phase2.close()

        xt = [t[:] for t in xt_own] + [
            t[:].rearrange("p c t -> p (c t)")[:, 0:Q * (P + 2)].rearrange("p (q n) -> p q n", q=Q)
            for t in (x1_hi, x1_lo)]
        conv_part = b_buf
        ffn_f = mix[:].rearrange("p g q -> p (g q)")
        ffn_q = agg_b[:, 0:TOKENS // 2].bitcast(BF16)
        w_abs16 = agg_b[:, TOKENS // 2:TOKENS // 2 + H // 2].bitcast(BF16)
        w_m16 = agg_b[:, TOKENS // 2 + H // 2:TOKENS // 2 + H].bitcast(BF16)
        w_plus = agg_b[:, TOKENS // 2 + H:TOKENS // 2 + 2 * H]

        cond_in = sem("cond_in")
        mixw_in = sem("mixw_in")
        x_in = [sem(f"x_in{t}") for t in range(TILES)]
        lr_in = sem("lr_in")
        lrb_in = [sem(f"lrb_in{m}") for m in range(2)]
        scale_in = sem("scale_in")
        down_in = sem("down_in")
        conv_in = sem("conv_in")
        q_in = [sem(f"q_in{n}") for n in range(RING)]
        ffn_in = sem("ffn_in")
        out_done = [sem(f"out_done{n}") for n in range(2)]
        const_set = sem("const_set")
        mix_zero = sem("mix_zero")
        h0_mm, h0_act = sem("h0_mm"), sem("h0_act")
        h1_mm, h1_act = sem("h1_mm"), sem("h1_act")
        logit_mm = sem("logit_mm")
        soft = sem("soft")
        exp_done = sem("exp_done")
        att_tr = sem("att_tr")
        att_ready = sem("att_ready")
        mix_mm = sem("mix_mm")
        mix_ready = sem("mix_ready")
        aggb_mm, aggb_ready = sem("aggb_mm"), sem("aggb_ready")
        ctx_mm, ctx_sum, ctx_full = sem("ctx_mm"), sem("ctx_sum"), sem("ctx_full")
        ctx_hi, ctx_ready = sem("ctx_hi"), sem("ctx_ready")
        q_ready = sem("q_ready")
        scale_ready = sem("scale_ready")
        lra_hi, lra_ready = sem("lra_hi"), sem("lra_ready")
        lrb_hi, lrb_ready = sem("lrb_hi"), sem("lrb_ready")
        down_hi, down_ready = sem("down_hi"), sem("down_ready")
        conv_hi, conv_ready = sem("conv_hi"), sem("conv_ready")
        cond_mm = sem("cond_mm")
        xs_ready = sem("xs_ready")
        x1_hi_ready, x1_lo_ready = sem("x1_hi_ready"), sem("x1_lo_ready")
        p_mm, p_hi_ready, p_lo_ready = sem("p_mm"), sem("p_hi_ready"), sem("p_lo_ready")
        sel_mm, t4_hi_ready, t4_lo_ready = sem("sel_mm"), sem("t4_hi_ready"), sem("t4_lo_ready")
        q_mm, l_mm = sem("q_mm"), sem("l_mm")
        ag_ready, au_ready = sem("ag_ready"), sem("au_ready")
        g_ready, u_ready = sem("g_ready"), sem("u_ready")
        silu_ready, h_ready = sem("silu_ready"), sem("h_ready")
        h_hi_ready, h_lo_ready = sem("h_hi_ready"), sem("h_lo_ready")
        down_mm = sem("down_mm")
        pd_mm, pd_hi_ready, pd_lo_ready = sem("pd_mm"), sem("pd_hi_ready"), sem("pd_lo_ready")
        seld_mm = sem("seld_mm")
        t4d_hi_ready, t4d_lo_ready = sem("t4d_hi_ready"), sem("t4d_lo_ready")
        down_l_mm = sem("down_l_mm")
        yq_ready, y_ready, x2_ready = sem("yq_ready"), sem("y_ready"), sem("x2_ready")
        stage_hi_ready, stage_lo_ready = sem("stage_hi_ready"), sem("stage_lo_ready")
        stored = sem("stored")
        xt_in = [sem(f"xt_in{n}") for n in range(XT)]
        xt_zero = sem("xt_zero")
        conv_mm, part_out, z_ready = sem("conv_mm"), sem("part_out"), sem("z_ready")
        amax_ready = sem("amax_ready")
        wmax, w_diag, w_row_mm, w_steps = sem("wmax"), sem("w_diag"), sem("w_row_mm"), sem("w_steps")
        xmax, x_diag, x_row_mm, x_steps = sem("xmax"), sem("x_diag"), sem("x_row_mm"), sem("x_steps")
        x_scale_ready = sem("x_scale_ready")
        v_ready, m_ready = sem("v_ready"), sem("m_ready")
        w_abs = sem("w_abs")
        wq_step = sem("wq_step")
        wmax_part = sem("wmax_part")
        v_plus_ready = sem("v_plus_ready")
        q_raw_ready, q_own_ready = sem("q_raw_ready"), sem("q_own_ready")
        q_fp8_ready = sem("q_fp8_ready")
        ffn_mm, o_ready = sem("ffn_mm"), sem("o_ready")

        slots = [("gate", ic) if m == 0 else ("up", ic) for ic in range(IC) for m in range(2)]
        slots += [("down", ic) for ic in range(IC)]

        def slot_width(n):
            kind, ic = slots[n]
            return H if kind == "down" else HC * width(ic)

        def slot(n):
            return x_nat[:, GROUPS - RING + n % RING, 0:slot_width(n)].bitcast(I32)

        def slot_dram(n):
            kind, ic = slots[n]
            a = {"gate": gate_q, "up": up_q, "down": down_q}[kind]
            return a[:, H * ic:H * ic + slot_width(n)]

        def slot_weights(n):
            kind, ic = slots[n]
            w = {"gate": gate_w[:], "up": up_w[:], "down": down_w[:].rearrange("p c n -> p (c n)")}[kind]
            return w[:, H * ic:H * ic + slot_width(n)]

        def bank(ic, n):
            return 4 * (ic % 2) + n

        split_buf = [a_buf[:, 1, :], b_buf[:, 1, :], a_buf[:, 0, :], b_buf[:, 0, :]]
        p_hi, p_lo = h_hi[:, IC - 2, :], h_lo[:, IC - 2, :]
        t4 = [h_hi[:, IC - 1, :], h_lo[:, IC - 1, :]]

        steps = [(sum(STEPS[:n]), k) for n, k in enumerate(STEPS)]

        def by_chunk(ap, k):
            return ap[:, 0:k * H].rearrange("p (c q) -> p c q", c=HC)

        def conv_out(g, part):
            banks = ps[:, 2 * (g % 2):2 * (g % 2) + 2, :].rearrange("p k (b m n) -> p (k b) m n", b=2, m=2)
            return banks[:, :, part, :]

        def plain(ap):
            return ap.bitcast(F32)

        def x_tile(dram, t):
            return dram[t * TILE:(t + 1) * TILE, :].rearrange("(g p) h -> p g h", p=P)

        def spread_mix(copy, q, args):
            for b in range(GB):
                src = ps[q * S:(q + 1) * S, 5, :].rearrange("p (o g b) -> p b g o", g=GROUPS, b=GB)[:, b]
                dst = mix[b * S:(b + 1) * S, :, b * S:(b + 1) * S].rearrange("p g (o q) -> p q g o", q=OB)[:, q]
                last = copy(dst, src, *args)
            return last

        block = ctx.enter_context(nc.Block())

        @block.sync
        def _(sp):
            sp.dma_start(cond_in_sb[:], cond_pack).then_inc(cond_in, 16)
            sp.dma_start(cond_w_sb[:].rearrange("k o p -> k (o p)"), cond_w).then_inc(mixw_in, 16)
            sp.dma_start(bias_k_sb[:], bias_k).then_inc(mixw_in, 16)
            sp.dma_start(ident[:], ident_in).then_inc(lr_in, 16)
            sp.dma_start(stage_sel[:].rearrange("p m q -> p (m q)"), sel_in).then_inc(lr_in, 16)
            sp.dma_start(stage_lr_a[:].rearrange("p c m r -> p (c m r)"), lr_a).then_inc(lr_in, 16)
            sp.dma_start(x_nat[:, 0:TG, :], x_tile(x, 0)).then_inc(x_in[0], 16)

            def load_slot(n):
                if n >= RING:
                    sp.wait_ge(q_ready, n - RING + 1)
                sp.dma_start(slot(n), slot_dram(n)).then_inc(q_in[n % RING], 16)

            sp.dma_start(stage_gate_b[:], gate_b).then_inc(lrb_in[0], 16)
            for n in range(2):
                load_slot(n)
            sp.dma_start(stage_up_b[:], up_b).then_inc(lrb_in[1], 16)
            for n in range(2, 4):
                load_slot(n)
            sp.dma_start(gate_sc[:], gate_s).then_inc(scale_in, 16)
            sp.dma_start(up_sc[:], up_s).then_inc(scale_in, 16)
            for n in range(4, RING):
                load_slot(n)
            sp.dma_start(down_sb[:], down_s).then_inc(down_in, 16)
            sp.dma_start(stage_down_a[:].rearrange("p c r -> p (c r)"), down_a).then_inc(down_in, 16)
            sp.dma_start(stage_down_b[:], down_b).then_inc(down_in, 16)
            sp.dma_start(stage_conv[:].rearrange("p s n -> p (s n)"), conv_w).then_inc(conv_in, 16)
            sp.dma_start(stage_mask[:], batch_mask).then_inc(conv_in, 16)
            sp.dma_start(stage_side[:], fside).then_inc(conv_in, 16)
            sp.dma_start(stage_ctx_w[:], ctx_w).then_inc(conv_in, 16)
            for n in range(RING, 2 * IC):
                load_slot(n)
            sp.dma_start(x_nat[:, TG:2 * TG, :], x_tile(x, 1)).then_inc(x_in[1], 16)
            for n in range(2 * IC, 3 * IC):
                load_slot(n)
            sp.wait_ge(q_ready, 3 * IC)
            for t in range(2, TILES):
                sp.dma_start(x_nat[:, t * TG:(t + 1) * TG, :], x_tile(x, t)).then_inc(x_in[t], 16)

            def store(g):
                sp.wait_ge(stage_hi_ready, g + 1)
                sp.wait_ge(stage_lo_ready, g + 1)
                sp.dma_start(turned[g].rearrange("m p h -> p m h"), plain(stage[:])).then_inc(stored, 16)

            def load(g):
                sp.wait_ge(stored, 16 * (g + 1))
                if g < XT:
                    sp.wait_ge(q_mm, 2 * TILES * IC)
                    sp.wait_ge(xt_zero, XT)
                else:
                    sp.wait_ge(conv_mm, g - XT + 1)
                sp.dma_start(plain(xt[g % XT][:, :, 1:P + 1]),
                             turned[g].rearrange("m (b c) (k n) -> (c k) (m b) n", b=GB, n=P)).then_inc(xt_in[g % XT], 16)

            for g in range((TILES - 1) * TG):
                if g == (TILES - 1) * TG - 1:
                    sp.wait_ge(cond_mm, TILES * HC)
                    sp.dma_start(ffn_f, ffn_w).then_inc(ffn_in, 16)
                store(g)
            for g in range(XT):
                load(g)
            for j in range(TG):
                for g in range(CONV_FROM[j] + XT, min(CONV_FROM[j] + CONV_AFTER[j] + XT, GROUPS)):
                    if j == TG - 1 and g == GROUPS - 3:
                        store(GROUPS - 1)
                    load(g)
                if j < TG - 1:
                    store((TILES - 1) * TG + j)
            for n, (g, k) in enumerate(steps):
                sp.wait_ge(o_ready, n + 1)
                sp.dma_start(out[g * P:(g + k) * P, :].rearrange("(k p) h -> p k h", p=P),
                             o_buf[:, n % 2, 0:k * H].rearrange("p (k h) -> p k h", k=k)).then_inc(out_done[n % 2], 16)
            for n in range(2):
                sp.wait_ge(out_done[n], 16 * len(range(n, len(steps), 2)))

        @block.tensor
        def _(pe):
            mm = nc.tensor.matmul

            def keep_clock(n):
                for _ in range(n):
                    mm(ps[:, 7, 0:P], ones[:], ones[:], start=True, stop=True)

            pe.wait_ge(const_set, 1)
            keep_clock(WARM[0])
            pe.wait_ge(cond_in, 16)
            mm(ps[:, 0, 0:B], w0_sb, cond_sb, start=True, stop=True).then_inc(h0_mm, 1)
            keep_clock(WARM[1])
            pe.wait_ge(h0_act, 1)
            mm(ps[:, 1, 0:B], w1_sb, h0[:], start=True, stop=True).then_inc(h1_mm, 1)
            keep_clock(WARM[2])
            pe.wait_ge(h1_act, 1)
            mm(ps[0:B, 2, 0:EXPERTS], h1[:], w2_sb, start=True, stop=True).then_inc(logit_mm, 1)
            keep_clock(WARM[3])
            pe.wait_ge(soft, 4)
            pe.wait_ge(lr_in, 3 * 16)
            nc.tensor.transpose(ps[0:EXPERTS, 3, 0:B], att[:], ident[0:B, 0:B]).then_inc(att_tr, 1)
            pe.wait_ge(att_ready, 1)
            pe.wait_ge(mixw_in, 2 * 16)
            for o in range(S // OB):
                last = mm(ps[:, 5, o * B:(o + 1) * B], cond_w_sb[:, o, :], att_t[:], start=True, stop=True)
            last.then_inc(mix_mm, 1)

            def mixed_bias(t):
                mm(ps[:, BIAS_BANK[t], :], ones[0:EXPERTS, :],
                   att_bias[:].rearrange("k b s -> k (b s)")[:, t * TILE:(t + 1) * TILE],
                   start=True, stop=True).then_inc(aggb_mm, 1)

            pe.wait_ge(att_ready, 2)
            mixed_bias(0)

            def condition(t):
                pe.wait_ge(x_in[t], 16)
                for c in range(HC):
                    for g in range(t * TG, (t + 1) * TG):
                        last = mm(ps[:, c, (g % TG) * P:(g % TG + 1) * P], x_nat[:, g, c * P:(c + 1) * P],
                                  mix[:, g, :], start=True, stop=True)
                    last.then_inc(cond_mm, 1)
                    yield

            def down_repeat(t):
                pe.wait_ge(pd_hi_ready, t + 1)
                pe.wait_ge(pd_lo_ready, t + 1)
                mm(ps[:, 7, :], sel[0:2 * R, 0, :], pd_hi[:], start=True, stop=False)
                mm(ps[:, 7, :], sel[0:2 * R, 0, :], pd_lo[:], start=False, stop=True).then_inc(seld_mm, 1)

            def down_low_rank(t, j):
                if j == 0:
                    pe.wait_ge(t4d_hi_ready, t + 1)
                    pe.wait_ge(t4d_lo_ready, t + 1)
                mm(ps[:, 6 + j % 2, :], t4d[:, j * P:(j + 1) * P], down_b4[:],
                   start=True, stop=True).then_inc(down_l_mm, 1)

            def down(t, j):
                if j == 0:
                    pe.wait_ge(u_ready, t * IC + IC - 1)
                    if t == 0:
                        pe.wait_ge(down_ready, 1)
                if j >= 2:
                    pe.wait_ge(y_ready, t * TG + j - 1)
                for ic in range(IC):
                    k = width(ic)
                    if j == 0:
                        pe.wait_ge(h_lo_ready, t * IC + ic + 1)
                        if t == 0:
                            pe.wait_ge(q_ready, 2 * IC + ic + 1)
                    if j == 1 and ic == 3:
                        down_repeat(t)
                    if j == 1 and ic == 8:
                        down_low_rank(t, 0)
                    for part in (h_hi, h_lo):
                        first, end = ic == 0 and part is h_hi, ic == IC - 1 and part is h_lo
                        if j == 0:
                            low = mm(ps[0:2 * R, 6, :], down_a_w[0:k, ic].rearrange("p m r -> p (m r)"),
                                     part[0:k, ic, :], start=first, stop=end)
                        last = mm(ps[:, 4 + j % 2, :], part[0:k, ic, j * P:(j + 1) * P], down_w[0:k, ic, :],
                                  start=first, stop=end)
                if j == 0:
                    low.then_inc(pd_mm, 1)
                last.then_inc(down_mm, 1)
                if j > 0:
                    down_low_rank(t, j)

            def quantised(t, ic, m):
                if t == 0:
                    pe.wait_ge(q_ready, 2 * ic + m + 1)
                w = (gate_w, up_w)[m]
                k = width(ic)
                for c in range(HC):
                    for part in (x1_hi, x1_lo):
                        last = mm(ps[0:k, bank(ic, 2 * m), :], w[:, H * ic + c * k:H * ic + (c + 1) * k],
                                  part[:, c, :], start=c == 0 and part is x1_hi, stop=c == HC - 1 and part is x1_lo)
                last.then_inc(q_mm, 1)

            def low_rank(t, ic, m):
                w = (gate_b4, up_b4)[m]
                mm(ps[0:width(ic), bank(ic, 2 * m + 1), :], w[:, ic * P:ic * P + width(ic)], t4[m],
                   start=True, stop=True).then_inc(l_mm, 1)

            def spread(diagonal, to, mm_sem):
                pe.wait_ge(diagonal, 1)
                mm(ps[:, to, 0:P], ones[:], diag[:], start=True, stop=True).then_inc(mm_sem, 1)

            def convolve(g):
                pe.wait_ge(xt_in[g % XT], 16 * (g // XT + 1))
                if g == 0:
                    pe.wait_ge(conv_ready, 1)
                    pe.wait_ge(ctx_ready, 2)
                    pe.wait_ge(u_ready, TILES * IC)
                if g >= 2:
                    pe.wait_ge(z_ready, g - 1)
                for b in range(GB):
                    to = ps[:, 2 * (g % 2) + b // 2, :]
                    if b % 2 == 0:
                        mm(to.rearrange("p (q f o) -> p q f o", q=4, f=PHASES),
                           ctx_pick[:, g:g + 1].to_broadcast([B, P]),
                           ctx_rhs[:, b:b + 2].rearrange("b q m o -> b (q m) o").unsqueeze(2)
                           .to_broadcast([B, 4, PHASES, S]), start=True, stop=False)
                    for k in range(SHIFTS):
                        for m in range(2):
                            last = mm(to[:, b % 2 * 2 * P:(b % 2 + 1) * 2 * P], xt[g % XT][:, m * GB + b, k:k + P],
                                      conv_wt[:, k].rearrange("p m n -> p (m n)"), start=False,
                                      stop=b % 2 == 1 and m == 1 and k == SHIFTS - 1)
                last.then_inc(conv_mm, 1)

            pe.wait_ge(mix_ready, 2)
            for _ in condition(0):
                pass

            def biases_and_context():
                pe.wait_ge(att_ready, 3)
                for t in range(1, TILES):
                    mixed_bias(t)
                pe.wait_ge(conv_in, 4 * 16)
                pe.wait_ge(aggb_ready, 1)
                mm(ps[0:B, 4, 0:S], cond_sb, stage_ctx_w[:], start=True, stop=True).then_inc(ctx_mm, 1)
                pe.wait_ge(aggb_ready, 3)

            for t in range(TILES):
                if t == 0:
                    pe.wait_ge(lra_ready, 1)
                for c in range(HC):
                    pe.wait_ge(x1_hi_ready, t * HC + c + 1)
                    pe.wait_ge(x1_lo_ready, t * HC + c + 1)
                    for part in (x1_hi, x1_lo):
                        last = mm(ps[:, bank(0, 1), :], lr_a_w[:, c].rearrange("p m v r -> p (m v r)"),
                                  part[:, c, :], start=c == 0 and part is x1_hi,
                                  stop=c == HC - 1 and part is x1_lo)
                last.then_inc(p_mm, 1)
                quantised(t, 0, 0)
                quantised(t, 0, 1)
                if t == 0:
                    biases_and_context()
                pe.wait_ge(p_hi_ready, t + 1)
                pe.wait_ge(p_lo_ready, t + 1)
                if t > 0:
                    pe.wait_ge(y_ready, t * TG)
                for m in range(2):
                    mm(ps[:, bank(1, 2 * m + 1), :], sel[:, m, :], p_hi, start=True, stop=False)
                    mm(ps[:, bank(1, 2 * m + 1), :], sel[:, m, :], p_lo, start=False, stop=True).then_inc(sel_mm, 1)
                if t == 0:
                    pe.wait_ge(lrb_ready, 2)
                for m in range(2):
                    if t == 0 and m == 0:
                        pe.wait_ge(ctx_sum, 1)
                    if t == 0 and m == 1:
                        pe.wait_ge(aggb_ready, TILES)
                    quantised(t, 1, m)
                    pe.wait_ge(t4_hi_ready, 2 * t + m + 1)
                    pe.wait_ge(t4_lo_ready, 2 * t + m + 1)
                    low_rank(t, 0, m)
                low_rank(t, 1, 0)
                low_rank(t, 1, 1)
                for ic in range(2, IC):
                    for m in range(2):
                        pe.wait_ge((g_ready, u_ready)[m], t * IC + ic - 1)
                        if t == TILES - 1 and ic == W_SPREAD and m == 0:
                            spread(w_diag, bank(ic, 1), w_row_mm)
                        quantised(t, ic, m)
                        if t == TILES - 1 and ic == W_SPREAD and m == 0:
                            pe.wait_ge(w_steps, 1)
                        low_rank(t, ic, m)
                for j in range(TG):
                    down(t, j)
                    if t + 1 < TILES and j == TG - 2:
                        for _ in condition(t + 1):
                            pass
                    if t == TILES - 1:
                        for n in range(CONV_AFTER[j]):
                            convolve(CONV_FROM[j] + n)
            spread(x_diag, 6, x_row_mm)
            pe.wait_ge(wq_step, W_STEPS * HC)
            for n, (g, k) in enumerate(steps):
                pe.wait_ge(q_fp8_ready, n + 1)
                if n >= 2:
                    pe.wait_ge(o_ready, n - 1)
                for j in range(k):
                    for c in range(HC):
                        last = mm(ps[:, 2 * (n % 2) + j, :], by_chunk(q_fp8[:, n % 2], k)[:, c, j * P:(j + 1) * P],
                                  ffn_q[:, c * H:(c + 1) * H], start=c == 0, stop=c == HC - 1)
                last.then_inc(ffn_mm, 1)

        @block.scalar
        def _(act):
            copy, activation = ACT.Copy, nc.scalar.activation
            act.wait_ge(cond_in, 16)
            act.wait_ge(h0_mm, 1)
            activation(h0[:], ps[:, 0, 0:B], ACT.Gelu, bias=b0_sb).then_inc(h0_act, 1)
            act.wait_ge(h1_mm, 1)
            activation(h1[:], ps[:, 1, 0:B], ACT.Gelu, bias=b1_sb).then_inc(h1_act, 1)
            act.wait_ge(soft, 2)
            activation(probs[:], logits[:], ACT.Exp, bias=stat[:, 0:1], accum_out=stat[:, 1:2]).then_inc(exp_done, 1)
            act.wait_ge(lr_in, 3 * 16)
            activation(sel[:], stage_sel[:], copy)
            activation(lr_a_w[:, :, :, 0, :], stage_lr_a[:], copy).then_inc(lra_hi, 1)
            act.wait_ge(mix_mm, 1)
            act.wait_ge(mix_zero, 1)
            for q in range(2, OB):
                last = spread_mix(activation, q, (copy,))
            last.then_inc(mix_ready, 1)
            def split_mixed(t):
                for c in range(HC):
                    act.wait_ge(xs_ready, t * HC + c + 1)
                    activation(x1_hi[:, c, :], split_buf[c], copy).then_inc(x1_hi_ready, 1)

            def keep_bias(t):
                act.wait_ge(aggb_mm, t + 1)
                activation(agg_b[:, t * TILE:(t + 1) * TILE], ps[:, BIAS_BANK[t], :], copy).then_inc(aggb_ready, 1)

            keep_bias(0)
            act.wait_ge(lrb_in[0], 16)
            activation(gate_b4[:], stage_gate_b[:], copy).then_inc(lrb_hi, 1)
            split_mixed(0)
            act.wait_ge(lrb_in[1], 16)
            activation(up_b4[:], stage_up_b[:], copy).then_inc(lrb_hi, 1)
            act.wait_ge(p_mm, 1)
            activation(p_hi, ps[:, bank(0, 1), :], copy, scale=LR_SCALE).then_inc(p_hi_ready, 1)
            act.wait_ge(down_in, 3 * 16)
            activation(down_a_w[:, :, 0, :], stage_down_a[:], copy).then_inc(down_hi, 1)
            activation(down_b4[:], stage_down_b[:], copy).then_inc(down_hi, 1)
            for t in range(1, TILES):
                keep_bias(t)
            act.wait_ge(conv_in, 4 * 16)
            activation(conv_wt[:, :, 0, :], stage_conv[:], copy).then_inc(conv_hi, 1)
            activation(ctx_pick[:], stage_mask[:, GB:], copy).then_inc(ctx_ready, 1)

            def context_high():
                act.wait_ge(ctx_full, 1)
                activation(ctx_rhs[:, :, 0, :], y_buf[0:B, 1, 0:P].rearrange("b (q o) -> b q o", q=GB),
                           copy).then_inc(ctx_hi, 1)

            def down_high(t):
                act.wait_ge(pd_mm, t + 1)
                activation(pd_hi[:], ps[0:2 * R, 6, :], copy, scale=LR_SCALE).then_inc(pd_hi_ready, 1)
                yield
                act.wait_ge(seld_mm, t + 1)
                activation(t4d[:], ps[:, 7, :], copy).then_inc(t4d_hi_ready, 1)
                yield

            def h_high(t, ic):
                n = t * IC + ic
                act.wait_ge(h_ready, n + 1)
                k = width(ic)
                activation(h_hi[0:k, ic, :], a_buf[0:k, ic % 2, :], copy).then_inc(h_hi_ready, 1)

            def stage_high(g):
                act.wait_ge(x2_ready, g + 1)
                if g > 0:
                    act.wait_ge(stored, 16 * g)
                activation(stage[:, 0, :], x_nat[:, g, :], copy).then_inc(stage_hi_ready, 1)

            def conv_low(g):
                act.wait_ge(conv_mm, g + 1)
                if g == 0:
                    act.wait_ge(h_ready, TILES * IC)
                if g >= 2:
                    act.wait_ge(z_ready, g - 1)
                activation(conv_part[:, g % 2, :].rearrange("p (b n) -> p b n", b=GB), conv_out(g, 1),
                           copy).then_inc(part_out, 1)

            for t in range(TILES):
                if t > 0:
                    act.wait_ge(p_mm, t + 1)
                    activation(p_hi, ps[:, bank(0, 1), :], copy, scale=LR_SCALE).then_inc(p_hi_ready, 1)
                else:
                    act.wait_ge(scale_ready, 2)
                for ic in range(IC):
                    n = t * IC + ic
                    k = width(ic)
                    act.wait_ge(q_mm, 2 * n + 1)
                    if ic >= 2:
                        act.wait_ge(h_lo_ready, n - 1)
                    activation(a_buf[0:k, ic % 2, :], ps[0:k, bank(ic, 0), :], copy,
                               scale=gate_sc[0:k, ic:ic + 1]).then_inc(ag_ready, 1)
                    act.wait_ge(q_mm, 2 * n + 2)
                    activation(b_buf[0:k, ic % 2, :], ps[0:k, bank(ic, 2), :], copy,
                               scale=up_sc[0:k, ic:ic + 1]).then_inc(au_ready, 1)
                    if ic == 0:
                        for m in range(2):
                            act.wait_ge(sel_mm, 2 * t + m + 1)
                            activation(t4[m], ps[:, bank(1, 2 * m + 1), :], copy).then_inc(t4_hi_ready, 1)
                    if ic >= 1:
                        h_high(t, ic - 1)
                    if ic == 3 and t > 0:
                        stage_high(t * TG - 1)
                    if ic == 1 and t == 0:
                        context_high()
                    act.wait_ge(g_ready, n + 1)
                    activation(a_buf[0:k, ic % 2, :], a_buf[0:k, ic % 2, :], ACT.Silu).then_inc(silu_ready, 1)
                    if t == TILES - 1 and 5 <= ic < 5 + HC:
                        c = ic - 5
                        if c == 0:
                            act.wait_ge(w_steps, 5)
                        else:
                            act.wait_ge(wq_step, (c - 1) * W_STEPS + 1)
                        activation(w_abs16, ffn_f[:, c * H:(c + 1) * H], ACT.Abs,
                                   scale=small[:, 19:20]).then_inc(w_abs, 1)
                h_high(t, IC - 1)
                high = down_high(t)
                next(high)
                for j in range(TG):
                    last_tile = t == TILES - 1
                    if j == 2 and not last_tile:
                        split_mixed(t + 1)
                    if last_tile and j < TG - 1:
                        for n in range(CONV_AFTER[j] if j == 0 else 1):
                            conv_low(CONV_FROM[j] + n)
                    if j == 0:
                        next(high)
                    if j < TG - 1 or last_tile:
                        stage_high(t * TG + j)
                    if last_tile and j > 0:
                        for g in range(CONV_FROM[j] + (j < TG - 1), CONV_FROM[j] + CONV_AFTER[j]):
                            conv_low(g)
            act.wait_ge(x_scale_ready, 1)
            for n, (g, k) in enumerate(steps):
                if n >= 2:
                    act.wait_ge(m_ready, n - 1)
                activation(by_chunk(v16[:, n % 2], k), t_t[:, :, g * P:(g + k) * P], ACT.Abs,
                           scale=small[:, 15:16]).then_inc(v_ready, 1)

        @block.gpsimd
        def _(pool):
            nc.gpsimd.memset(mix[:], 0.0).then_inc(mix_zero, 1)
            for m, (w, st) in enumerate(((gate_b4, stage_gate_b), (up_b4, stage_up_b))):
                pool.wait_ge(lrb_hi, m + 1)
                for q in (1, 3):
                    rows = slice(q * S, (q + 1) * S)
                    last = nc.gpsimd.tensor_tensor(w[rows, :], st[rows, :], plain(w[rows, :]), ALU.subtract)
                last.then_inc(lrb_ready, 1)

            def stage_low(g):
                pool.wait_ge(stage_hi_ready, g + 1)
                nc.gpsimd.tensor_tensor(stage[:, 1, :], x_nat[:, g, :], plain(stage[:, 0, :]),
                                        ALU.subtract).then_inc(stage_lo_ready, 1)

            for t in range(TILES):
                for ic in range(IC):
                    n = t * IC + ic
                    k = width(ic)
                    pool.wait_ge(h_hi_ready, n + 1)
                    nc.gpsimd.tensor_tensor(h_lo[0:k, ic, :], a_buf[0:k, ic % 2, :], plain(h_hi[0:k, ic, :]),
                                            ALU.subtract).then_inc(h_lo_ready, 1)
                    if ic == 3 and t > 0:
                        stage_low(t * TG - 1)
                for j in range(TG if t + 1 < TILES else TG - 1):
                    n = t * TG + j
                    pool.wait_ge(y_ready, n + 1)
                    nc.gpsimd.tensor_tensor(x_nat[:, n, :], y_buf[:, j % 2, :], x_nat[:, n, :],
                                            ALU.add).then_inc(x2_ready, 1)
                    if j < TG - 1:
                        stage_low(n)
            for n, (g, k) in enumerate(steps):
                if k == 1:
                    continue
                pool.wait_ge(v_plus_ready, n + 1)
                if n >= 2:
                    pool.wait_ge(q_fp8_ready, n - 1)
                nc.gpsimd.tensor_tensor(q_raw[:, n % 2, 0:k * H], v_plus[:, n % 2, 0:k * H], m16[:, n % 2, 0:k * H],
                                        ALU.subtract).then_inc(q_raw_ready, 1)

        @block.vector
        def _(dve):
            v = nc.vector
            v.memset(ones[:], 1.0).then_inc(const_set, 1)
            dve.wait_ge(cond_in, 16)
            dve.wait_ge(logit_mm, 1)
            v.tensor_tensor(logits[:], ps[0:B, 2, 0:EXPERTS], b2_sb, ALU.add).then_inc(soft, 1)
            dve.wait_ge(soft, 1)
            v.tensor_reduce(stat[:, 0:1], logits[:], AX_X, ALU.max, negate=True).then_inc(soft, 1)
            dve.wait_ge(exp_done, 1)
            v.reciprocal(stat[:, 2:3], stat[:, 1:2]).then_inc(soft, 1)
            dve.wait_ge(soft, 3)
            v.tensor_scalar(att[:], probs[:], stat[:, 2:3], None, ALU.mult).then_inc(soft, 1)
            dve.wait_ge(att_tr, 1)
            v.tensor_copy(att_t[:], ps[0:EXPERTS, 3, 0:B]).then_inc(att_ready, 1)
            dve.wait_ge(att_ready, 1)
            dve.wait_ge(mixw_in, 2 * 16)

            def expert_bias(b0, b1):
                v.tensor_tensor(att_bias[:, b0:b1], att_t[:, b0:b1].unsqueeze(2).to_broadcast([EXPERTS, b1 - b0, S]),
                                bias_k_sb[:].unsqueeze(1).to_broadcast([EXPERTS, b1 - b0, S]),
                                ALU.mult).then_inc(att_ready, 1)

            expert_bias(0, TILE // S)
            dve.wait_ge(mix_mm, 1)
            dve.wait_ge(mix_zero, 1)
            for q in range(2):
                last = spread_mix(v.tensor_copy, q, ())
            last.then_inc(mix_ready, 1)

            def convert(n):
                dve.wait_ge(q_in[n % RING], 16 * (n // RING + 1))
                v.tensor_scalar(slot_weights(n), slot(n), Q_ZERO, None, ALU.subtract).then_inc(q_ready, 1)

            def split_mixed(t):
                for c in range(HC):
                    dve.wait_ge(cond_mm, t * HC + c + 1)
                    v.tensor_tensor(split_buf[c], ps[:, c, :], agg_b[:, t * TILE:(t + 1) * TILE],
                                    ALU.add).then_inc(xs_ready, 1)
                    if c > 0:
                        split_low(t, c - 1)
                split_low(t, HC - 1)

            def split_low(t, c):
                dve.wait_ge(x1_hi_ready, t * HC + c + 1)
                v.tensor_tensor(x1_lo[:, c, :], split_buf[c], plain(x1_hi[:, c, :]),
                                ALU.subtract).then_inc(x1_lo_ready, 1)

            def x_a_low(t):
                dve.wait_ge(p_hi_ready, t + 1)
                v.scalar_tensor_tensor(p_lo, ps[:, bank(0, 1), :], LR_SCALE, plain(p_hi), ALU.mult,
                                       ALU.subtract).then_inc(p_lo_ready, 1)

            dve.wait_ge(lra_hi, 1)
            v.tensor_tensor(lr_a_w[:, :, :, 1, :], stage_lr_a[:], plain(lr_a_w[:, :, :, 0, :]),
                            ALU.subtract).then_inc(lra_ready, 1)
            convert(0)
            convert(1)
            dve.wait_ge(aggb_ready, 1)
            split_mixed(0)
            expert_bias(TILE // S, B)
            dve.wait_ge(scale_in, 2 * 16)
            v.tensor_scalar(gate_sc[:], gate_sc[:], Q_STEP, None, ALU.mult).then_inc(scale_ready, 1)
            v.tensor_scalar(up_sc[:], up_sc[:], Q_STEP, None, ALU.mult).then_inc(scale_ready, 1)
            x_a_low(0)
            convert(2)
            convert(3)
            dve.wait_ge(down_hi, 2)
            v.tensor_tensor(down_a_w[:, :, 1, :], stage_down_a[:], plain(down_a_w[:, :, 0, :]), ALU.subtract)
            for q in (1, 3):
                rows = slice(q * S, (q + 1) * S)
                v.tensor_tensor(down_b4[rows, :], stage_down_b[rows, :], plain(down_b4[rows, :]), ALU.subtract)
            dve.wait_ge(down_in, 3 * 16)
            v.tensor_scalar(down_sb[:], down_sb[:], Q_STEP, None, ALU.mult).then_inc(down_ready, 1)
            dve.wait_ge(conv_hi, 1)
            v.tensor_tensor(conv_wt[:, :, 1, :], stage_conv[:], plain(conv_wt[:, :, 0, :]),
                            ALU.subtract).then_inc(conv_ready, 1)
            dve.wait_ge(conv_in, 4 * 16)
            dve.wait_ge(ctx_mm, 1)
            v.tensor_tensor(y_buf[0:B, 0, 0:S], ps[0:B, 4, 0:S], stage_side[:], ALU.add).then_inc(ctx_sum, 1)
            dve.wait_ge(ctx_sum, 1)
            v.tensor_tensor(y_buf[0:B, 1, 0:P].rearrange("p (b o) -> p b o", b=GB),
                            y_buf[0:B, 0, 0:S].unsqueeze(1).to_broadcast([B, GB, S]),
                            stage_mask[:, 0:GB].unsqueeze(2).to_broadcast([B, GB, S]), ALU.mult).then_inc(ctx_full, 1)

            def context_low():
                dve.wait_ge(ctx_hi, 1)
                v.tensor_tensor(ctx_rhs[:, :, 1, :], y_buf[0:B, 1, 0:P].rearrange("b (q o) -> b q o", q=GB),
                                plain(ctx_rhs[:, :, 0, :]), ALU.subtract).then_inc(ctx_ready, 1)

            def down_scaled(t, j):
                n = t * TG + j
                dve.wait_ge(down_mm, n + 1)
                if n >= 2:
                    dve.wait_ge(x2_ready, n - 1)
                v.tensor_tensor(y_buf[:, j % 2, :], ps[:, 4 + j % 2, :], down_sb[:], ALU.mult).then_inc(yq_ready, 1)

            def down_parts_low(t):
                dve.wait_ge(pd_hi_ready, t + 1)
                v.scalar_tensor_tensor(pd_lo[:], ps[0:2 * R, 6, :], LR_SCALE, plain(pd_hi[:]), ALU.mult,
                                       ALU.subtract).then_inc(pd_lo_ready, 1)

            def down_low(t):
                dve.wait_ge(t4d_hi_ready, t + 1)
                v.tensor_tensor(t4d[64:P, :], ps[64:P, 7, :], plain(t4d[64:P, :]), ALU.subtract).then_inc(
                    t4d_lo_ready, 1)

            def down_sum(t, j):
                n = t * TG + j
                dve.wait_ge(down_l_mm, n + 1)
                dve.wait_ge(yq_ready, n + 1)
                v.tensor_tensor(y_buf[:, j % 2, :], ps[:, 6 + j % 2, :], y_buf[:, j % 2, :],
                                ALU.add).then_inc(y_ready, 1)

            def diagonal(col, largest, done):
                dve.wait_ge(largest, 1)
                v.tensor_scalar(diag[:], ident[:], amax[:, col:col + 1], None, ALU.mult).then_inc(done, 1)

            def scale_from(row_mm, at, to, steps_done):
                largest, inverse = small[:, to:to + 1], small[:, to + 1:to + 2]
                dve.wait_ge(row_mm, 1)
                v.tensor_reduce(largest, ps[:, at, 0:P], AX_X, ALU.max).then_inc(steps_done, 1)
                dve.wait_ge(steps_done, 1)
                v.tensor_scalar(largest, largest, AMAX_MIN, None, ALU.max).then_inc(steps_done, 1)
                dve.wait_ge(steps_done, 2)
                v.reciprocal(inverse, largest).then_inc(steps_done, 1)
                dve.wait_ge(steps_done, 3)

            def weight_max(c):
                dve.wait_ge(ffn_in, 16)
                v.tensor_reduce(amax[:, WMAX + c:WMAX + c + 1], ffn_f[:, c * H:(c + 1) * H], AX_X, ALU.max,
                                apply_absolute_value=True).then_inc(wmax_part, 1)

            def weight_largest():
                dve.wait_ge(wmax_part, HC)
                v.tensor_reduce(amax[:, XMAX + 1:XMAX + 2], amax[:, WMAX:WMAX + HC], AX_X, ALU.max).then_inc(wmax, 1)
                diagonal(XMAX + 1, wmax, w_diag)

            def weight_scale():
                scale_from(w_row_mm, bank(W_SPREAD, 1), 4, w_steps)
                v.tensor_scalar(small[:, 18:19], small[:, 5:6], FP8_MAX, None, ALU.mult).then_inc(w_steps, 1)
                v.tensor_scalar(small[:, 19:20], small[:, 5:6], FP8_MAX, ROUND_SCALE, ALU.mult,
                                ALU.mult).then_inc(w_steps, 1)
                dve.wait_ge(w_steps, 5)

            def round_weight(n):
                c = n // W_STEPS
                w, scale = ffn_f[:, c * H:(c + 1) * H], small[:, 18:19]
                if n > 0:
                    dve.wait_ge(wq_step, n)
                if n % W_STEPS == 0:
                    dve.wait_ge(w_abs, c + 1)
                (lambda: v.tensor_scalar(w_m16, w_abs16, ROUND_MIN, None, ALU.max),
                 lambda: v.scalar_tensor_tensor(w_plus, w, scale, w_m16, ALU.mult, ALU.add),
                 lambda: v.tensor_tensor(w_m16, w_plus, w_m16, ALU.subtract),
                 lambda: v.tensor_scalar(ffn_q[:, c * H:(c + 1) * H], w_m16, FP8_MAX, -FP8_MAX, ALU.min,
                                         ALU.max))[n % W_STEPS]().then_inc(wq_step, 1)

            def conv_sum(g):
                dve.wait_ge(part_out, g + 1)
                if g == 0:
                    dve.wait_ge(q_mm, 2 * TILES * IC)
                v.tensor_tensor(t_t[:, :, g * P:(g + 1) * P].rearrange("p f (b o) -> p b f o", b=GB),
                                conv_out(g, 0).rearrange("p b (f o) -> p b f o", f=PHASES),
                                conv_part[:, g % 2, :].rearrange("p (b f o) -> p b f o", b=GB, f=PHASES),
                                ALU.add).then_inc(z_ready, 1)
                dve.wait_ge(z_ready, g + 1)
                v.tensor_reduce(amax[:, PHASES * g:PHASES * (g + 1)], t_t[:, :, g * P:(g + 1) * P], AX_X, ALU.max,
                                apply_absolute_value=True).then_inc(amax_ready, 1)

            for t in range(TILES):
                if t > 0:
                    x_a_low(t)
                for m in range(2):
                    dve.wait_ge(t4_hi_ready, 2 * t + m + 1)
                    v.tensor_tensor(t4[m][64:P], ps[64:P, bank(1, 2 * m + 1), :], plain(t4[m][64:P]),
                                    ALU.subtract).then_inc(t4_lo_ready, 1)
                for ic in range(IC):
                    n = t * IC + ic
                    k = width(ic)
                    a, b = a_buf[0:k, ic % 2, :], b_buf[0:k, ic % 2, :]
                    if t == 0 and ic == 2:
                        context_low()
                    if t == 0:
                        for later in range(2 * ic + 4, min(2 * ic + 6, 2 * IC)):
                            convert(later)
                        if 2 * ic + 4 >= 2 * IC:
                            for later in range(2 * IC + 2 * (ic - IC + 2), 2 * IC + 2 * (ic - IC + 3)):
                                convert(later)
                    dve.wait_ge(ag_ready, n + 1)
                    dve.wait_ge(l_mm, 2 * n + 1)
                    v.tensor_tensor(a, ps[0:k, bank(ic, 1), :], a, ALU.add).then_inc(g_ready, 1)
                    dve.wait_ge(au_ready, n + 1)
                    dve.wait_ge(l_mm, 2 * n + 2)
                    v.tensor_tensor(b, ps[0:k, bank(ic, 3), :], b, ALU.add).then_inc(u_ready, 1)
                    dve.wait_ge(silu_ready, n + 1)
                    dve.wait_ge(u_ready, n + 1)
                    v.tensor_tensor(a, a, b, ALU.mult).then_inc(h_ready, 1)
                    if t == TILES - 1:
                        if ic in (1, 2):
                            weight_max(2 * ic - 2)
                            weight_max(2 * ic - 1)
                        if ic == 3:
                            weight_largest()
                        if ic == W_SPREAD - 1:
                            weight_scale()
                        for n in range(3 * (ic - 5), min(3 * (ic - 4), W_STEPS * HC) if ic >= 5 else 3 * (ic - 5)):
                            round_weight(n)
                if t == 0:
                    for later in range(2 * IC + 4, 3 * IC):
                        convert(later)
                if t == TILES - 1:
                    dve.wait_ge(q_mm, 2 * TILES * IC)
                    for n in range(XT):
                        for at in (0, P + 1):
                            last = v.memset(plain(xt[n][:, :, at:at + 1]), 0.0)
                        last.then_inc(xt_zero, 1)
                down_parts_low(t)
                for j in range(TG):
                    down_scaled(t, j)
                    if j == 0:
                        if t == TILES - 1:
                            for n in range(CONV_AFTER[0]):
                                conv_sum(n)
                        down_low(t)
                    down_sum(t, j)
                    if j == 2 and t + 1 < TILES:
                        split_mixed(t + 1)
                    if t == TILES - 1 and 0 < j < TG - 1:
                        for n in range(CONV_AFTER[j]):
                            conv_sum(CONV_FROM[j] + n)
            n = GROUPS - 1
            dve.wait_ge(y_ready, n + 1)
            v.tensor_tensor(x_nat[:, n, :], y_buf[:, n % 2, :], x_nat[:, n, :], ALU.add).then_inc(x2_ready, 1)
            dve.wait_ge(stage_hi_ready, n + 1)
            v.tensor_tensor(stage[:, 1, :], x_nat[:, n, :], plain(stage[:, 0, :]),
                            ALU.subtract).then_inc(stage_lo_ready, 1)
            for g in range(CONV_FROM[-1], GROUPS):
                conv_sum(g)
            dve.wait_ge(amax_ready, GROUPS)
            v.tensor_reduce(amax[:, XMAX:XMAX + 1], amax[:, 0:XMAX], AX_X, ALU.max).then_inc(xmax, 1)
            diagonal(XMAX, xmax, x_diag)
            scale_from(x_row_mm, 6, 6, x_steps)
            v.tensor_scalar(small[:, 15:16], small[:, 7:8], FP8_MAX, ROUND_SCALE, ALU.mult,
                            ALU.mult).then_inc(x_scale_ready, 1)
            v.tensor_scalar(small[:, 16:17], small[:, 7:8], FP8_MAX, None, ALU.mult).then_inc(x_scale_ready, 1)
            v.tensor_scalar(small[:, 17:18], small[:, 6:7], 1.0 / FP8_MAX, None, ALU.mult).then_inc(x_scale_ready, 1)
            dve.wait_ge(x_scale_ready, 3)
            v.tensor_scalar(small[:, 17:18], small[:, 17:18], small[:, 4:5], 1.0 / FP8_MAX, ALU.mult,
                            ALU.mult).then_inc(x_scale_ready, 1)

            def subtract(n, k):
                dve.wait_ge(v_plus_ready, n + 1)
                v.tensor_tensor(q_raw[:, n % 2, 0:k * H], v_plus[:, n % 2, 0:k * H], m16[:, n % 2, 0:k * H],
                                ALU.subtract).then_inc(q_own_ready, 1)

            def wait_subtracted(n):
                own = steps[n][1] == 1
                dve.wait_ge(q_own_ready if own else q_raw_ready,
                            sum((k == 1) == own for _, k in steps[:n + 1]))

            def clip(n, k):
                wait_subtracted(n)
                if n >= 2:
                    dve.wait_ge(ffn_mm, n - 1)
                v.tensor_scalar(q_fp8[:, n % 2, 0:k * H], q_raw[:, n % 2, 0:k * H], FP8_MAX, -FP8_MAX,
                                ALU.min, ALU.max).then_inc(q_fp8_ready, 1)

            def output(n, g, k):
                if n == 0:
                    dve.wait_ge(x_scale_ready, 4)
                dve.wait_ge(ffn_mm, n + 1)
                if n >= 2:
                    dve.wait_ge(out_done[n % 2], 16 * (n // 2))
                banks = ps[:, 2 * (n % 2):2 * (n % 2) + k, :].rearrange("p k h -> p (k h)")
                v.scalar_tensor_tensor(o_buf[:, n % 2, 0:k * H], banks, small[:, 17:18],
                                       x_nat[:, g:g + k, :].rearrange("p k h -> p (k h)"),
                                       ALU.mult, ALU.add).then_inc(o_ready, 1)

            for n, (g, k) in enumerate(steps):
                v_step, m = v16[:, n % 2, 0:k * H], m16[:, n % 2, 0:k * H]
                dve.wait_ge(v_ready, n + 1)
                if n >= 2:
                    wait_subtracted(n - 2)
                v.tensor_scalar(m, v_step, ROUND_MIN, None, ALU.max).then_inc(m_ready, 1)
                dve.wait_ge(m_ready, n + 1)
                v.scalar_tensor_tensor(by_chunk(v_plus[:, n % 2], k), t_t[:, :, g * P:(g + k) * P], small[:, 16:17],
                                       by_chunk(m16[:, n % 2], k), ALU.mult, ALU.add).then_inc(v_plus_ready, 1)
                if k == 1:
                    subtract(n, k)
                    if n == 0:
                        clip(n, k)
                if n >= 2:
                    clip(n - 1, steps[n - 1][1])
                if n >= 2:
                    output(n - 2, *steps[n - 2])
            n = len(steps) - 1
            clip(n, steps[n][1])
            output(n - 1, *steps[n - 1])
            output(n, *steps[n])


def kernel(x, cond_128, fside_S_0, L0_cond_W0, L0_cond_b0, L0_cond_W1, L0_cond_b1, L0_cond_W2, L0_cond_b2,
           L0_cond_weight, L0_cond_bias_k, L0_ffn_gate_q, L0_ffn_gate_scale, L0_ffn_gate_A, L0_ffn_gate_B,
           L0_ffn_up_q, L0_ffn_up_scale, L0_ffn_up_A, L0_ffn_up_B, L0_ffn_down_q, L0_ffn_down_scale,
           L0_ffn_down_A, L0_ffn_down_B, L1_cond_weight, L1_cond_c_weight, L1_ffn_weight):
    import numpy as np
    import concourse.bacc as bacc
    from concourse.bass_utils import run_bass_kernel_spmd

    a = np.asarray
    order = np.arange(H).reshape(P, PHASES).T.reshape(-1)

    def chunked(w):
        w = a(w).T[order].reshape(HC, P, I)
        return np.concatenate([w[:, :, ic * P:ic * P + width(ic)].transpose(1, 0, 2).reshape(P, -1)
                               for ic in range(IC)], axis=1)

    def by_chunk(w):
        w = a(w)
        w = np.concatenate([w, np.zeros((IC * P - I,) + w.shape[1:], w.dtype)])
        return w.reshape(IC, P, -1).transpose(1, 0, 2).reshape(P, -1)

    def broadcast(w, n):
        return np.broadcast_to(a(w)[None, :], (n, len(w)))

    lr_a = np.stack([a(L0_ffn_gate_A)[order], a(L0_ffn_up_A)[order]], axis=1).reshape(HC, P, 2 * R).transpose(1, 0, 2)
    cond_pack = np.zeros((P, COND_COLS), np.float32)
    for at, w in zip(COND_AT, (a(cond_128).T, a(L0_cond_W0), a(L0_cond_W1), a(L0_cond_W2), a(L0_cond_b0)[:, None],
                               a(L0_cond_b1)[:, None], broadcast(L0_cond_b2, B))):
        cond_pack[:w.shape[0], at:at + w.shape[1]] = w
    w = a(L1_cond_weight)
    conv_w = np.zeros((S, PHASES, SHIFTS, PHASES, S), w.dtype)
    for c in range(S):
        same = slice(c // CG * CG, (c // CG + 1) * CG)
        for into in range(PHASES):
            for shift in range(SHIFTS):
                for of in range(PHASES):
                    tap = PHASES * (shift - 1) + into - of + PAD
                    if 0 <= tap < TAPS:
                        conv_w[c, into, shift, of, same] = w[same, c % CG, tap]
    row = np.arange(B)[:, None]
    batch_mask = np.concatenate([row % GB == np.arange(GB), row // GB == np.arange(GROUPS)],
                                axis=1).astype(np.float32)
    row, col = np.arange(P)[:, None], np.arange(2 * P)[None, :]
    sel = ((row % R == col % R) & (row // (2 * R) == col // P)).astype(np.float32)
    arrays = {
        "x": a(x).reshape(TOKENS, H)[:, order], "cond_pack": cond_pack,
        "cond_w": a(L0_cond_weight).reshape(EXPERTS, S * S), "bias_k": a(L0_cond_bias_k),
        "gate_q": chunked(L0_ffn_gate_q), "up_q": chunked(L0_ffn_up_q),
        "gate_s": by_chunk(L0_ffn_gate_scale), "up_s": by_chunk(L0_ffn_up_scale),
        "lr_a": lr_a.reshape(P, -1), "gate_b": np.tile(a(L0_ffn_gate_B), (4, 1)),
        "up_b": np.tile(a(L0_ffn_up_B), (4, 1)),
        "down_q": by_chunk(a(L0_ffn_down_q)[order].T), "down_s": broadcast(a(L0_ffn_down_scale)[order], P),
        "down_a": by_chunk(L0_ffn_down_A), "down_b": np.tile(a(L0_ffn_down_B)[:, order], (4, 1)),
        "conv_w": conv_w.reshape(P, -1), "ctx_w": a(L1_cond_c_weight).T,
        "fside": broadcast(fside_S_0, B),
        "ffn_w": a(L1_ffn_weight)[order][:, order].reshape(HC, P, H).transpose(1, 0, 2).reshape(P, -1),
        "batch_mask": batch_mask, "ident": np.eye(P, dtype=np.float32), "sel": sel,
    }
    arrays = {f"in_{k}": np.ascontiguousarray(v) for k, v in arrays.items()}
    nc = bacc.Bacc("TRN2", target_bir_lowering=False, num_devices=1, dynamic_dma_scratch_size=1024)
    aps = [nc.dram_tensor(k, v.shape, mybir.dt.from_np(v.dtype), kind="ExternalInput").ap()
           for k, v in arrays.items()]
    out = nc.dram_tensor("out", (TOKENS, H), F32, kind="ExternalOutput").ap()
    turned = nc.dram_tensor("turned", (GROUPS, 2, P, H), F32, kind="Internal").ap()
    build(nc, *aps, turned, out)
    r = run_bass_kernel_spmd(nc, [arrays], core_ids=[0])
    result = np.empty((TOKENS, H), np.float32)
    result[:, order] = r.results[0]["out"]
    return result.reshape(B, S, H)
```

```python
from contextlib import ExitStack

from concourse import mybir

F32 = mybir.dt.float32
F32R = mybir.dt.float32r
BF16 = mybir.dt.bfloat16
I32 = mybir.dt.int32
ACT = mybir.ActivationFunctionType
ALU = mybir.AluOpType
AX_X = mybir.AxisListType.X

P = 128
B, S, H = 64, 32, 512
TOKENS = B * S
I = 1376
R = 32
EXPERTS = 8
TAPS, PAD = 9, 4
CONV_GROUPS = 4
Q_ZERO, Q_STEP, LR_SCALE = 7.5, 0.005, 0.02
FP8_MAX, AMAX_MIN = 448.0, 1e-12

HC = H // P
IC = -(-I // P)
GROUPS = TOKENS // P
GB = P // S
TILE = 512
TILES = TOKENS // TILE
TG = TILE // P
PHASES = H // P
SHIFTS = 3
Q = 2 * GB
CG = S // CONV_GROUPS
STEPS = (1,) + (2,) * (GROUPS // 2 - 1) + (1,)
RING = 8
WARM = (5, 4, 1, 7, 4)
BIAS_BANK = (4, 5, 7, 6)
XT = 4
CONV_AFTER = (3, 3, 2, 8)
CONV_FROM = tuple(sum(CONV_AFTER[:j]) for j in range(TG))
XMAX, WMAX = PHASES * GROUPS, PHASES * GROUPS + 2
W_SPREAD = 5
W_EACH = 3
W_STEPS = 4
ROUND_SCALE, ROUND_MIN = 2.0 ** 20, 1.5 * 2.0 ** 14
COND_WIDTHS = (B, P, P, EXPERTS, 1, 1, EXPERTS)
COND_AT = tuple(sum(COND_WIDTHS[:n]) for n in range(len(COND_WIDTHS)))
COND_COLS = sum(COND_WIDTHS)
OB = P // S


def width(ic):
    return min(P, I - ic * P)


def build(nc, x, cond_pack, cond_w, bias_k, gate_q, up_q, gate_s, up_s,
          lr_a, gate_b, up_b, down_q, down_s, down_a, down_b, conv_w, ctx_w, fside, ffn_w,
          batch_mask, ident_in, sel_in, turned, out):
    with ExitStack() as ctx:
        def sb(name, shape, dt, stack=ctx):
            return stack.enter_context(nc.sbuf_tensor(name, shape, dt))

        def sem(name):
            return ctx.enter_context(nc.semaphore(name))

        ps = ctx.enter_context(nc.psum_tensor("ps", [P, 8, 512], F32))

        x_nat = sb("x_nat", [P, GROUPS, H], F32)
        conv_wt = sb("conv_wt", [P, SHIFTS, 2, P], F32R)
        ctx_rhs = sb("ctx_rhs", [P, GB, S], F32R)
        ctx_pick = sb("ctx_pick", [P, GROUPS], F32R)
        stage = sb("stage", [P, 2, H], F32R)
        diag = sb("diag", [P, P], F32)
        ident = sb("ident", [P, P], F32)
        ones = sb("ones", [P, P], F32)
        y_buf = sb("y_buf", [P, 2, H], F32)
        small = sb("small", [P, 9], F32)
        amax = sb("amax", [P, WMAX + HC], F32)
        x1_hi = sb("x1_hi", [P, HC, TILE], F32R)
        x1_lo = sb("x1_lo", [P, HC, TILE], F32R)
        down_w = sb("down_w", [P, IC, H], F32R)
        gate_b4 = sb("gate_b4", [P, I], F32R)
        up_b4 = sb("up_b4", [P, I], F32R)
        down_b4 = sb("down_b4", [P, H], F32R)
        lr_a_w = sb("lr_a_w", [P, HC, 2, 2, R], F32R)
        down_a_w = sb("down_a_w", [P, IC, 2, R], F32R)
        down_sb = sb("down_sb", [P, H], F32)
        agg_b = sb("agg_b", [P, TOKENS], F32)
        mix = sb("mix", [P, GROUPS, P], F32)
        a_buf = sb("a_buf", [P, 2, TILE], F32)
        b_buf = sb("b_buf", [P, 2, TILE], F32)
        sel = sb("sel", [P, P], F32R)
        gate_sc = sb("gate_sc", [P, IC], F32)
        up_sc = sb("up_sc", [P, IC], F32)
        pd = sb("pd", [P, TILE], F32R)
        t4d = sb("t4d", [P, TILE], F32R)
        phase1 = ExitStack()
        gate_w = sb("gate_w", [P, HC * I], F32R, phase1)
        up_w = sb("up_w", [P, HC * I], F32R, phase1)
        h_hi = sb("h_hi", [P, IC, TILE], F32R, phase1)
        h_lo = sb("h_lo", [P, IC, TILE], F32R, phase1)
        phase1.close()
        early = ExitStack()
        pad_gate = sb("pad_gate", [P, 2 * HC * I], F32, early)
        cond_in_sb = sb("cond_in_sb", [P, COND_COLS], F32, early)
        h0 = sb("h0", [P, B], F32, early)
        h1 = sb("h1", [P, B], F32, early)
        logits = sb("logits", [B, EXPERTS], F32, early)
        probs = sb("probs", [B, EXPERTS], F32, early)
        att = sb("att", [B, EXPERTS], F32, early)
        att_t = sb("att_t", [EXPERTS, B], F32, early)
        stat = sb("stat", [B, 4], F32, early)
        bias_k_sb = sb("bias_k_sb", [EXPERTS, S], F32, early)
        cond_w_sb = sb("cond_w_sb", [EXPERTS, S // OB, P], F32, early)
        att_bias = sb("att_bias", [EXPERTS, B, S], F32, early)
        stage_lr_a = sb("stage_lr_a", [P, HC, 2, R], F32, early)
        stage_sel = sb("stage_sel", [P, P], F32, early)
        stage_mask = sb("stage_mask", [P, GB + GROUPS], F32, early)
        stage_side = sb("stage_side", [P, S], F32, early)
        stage_ctx_w = sb("stage_ctx_w", [P, S], F32, early)
        used = 4 * (COND_COLS + 2 * B + 3 * EXPERTS + B + 4 + S + S // OB * P + B * S + HC * 2 * R + P
                    + GB + GROUPS + S + S)
        pad_h = sb("pad_h", [P, (4 * IC * TILE - used) // 4 + 32], F32, early)
        stage_gate_b = sb("stage_gate_b", [P, I], F32, early)
        stage_up_b = sb("stage_up_b", [P, I], F32, early)
        stage_down_b = sb("stage_down_b", [P, H], F32, early)
        stage_down_a = sb("stage_down_a", [P, IC, R], F32, early)
        stage_conv = sb("stage_conv", [P, SHIFTS, P], F32, early)
        early.close()
        cond_sb, w0_sb, w1_sb, w2_sb, b0_sb, b1_sb, b2_sb = (
            cond_in_sb[0:rows, COND_AT[n]:COND_AT[n] + COND_WIDTHS[n]]
            for n, rows in enumerate((P, P, P, P, P, P, B)))
        phase2 = ExitStack()
        t_t = sb("t_t", [P, HC, TOKENS], F32, phase2)
        xt_own = [sb(f"xt{n}", [P, Q, P + 2], F32R, phase2) for n in range(2)]
        pad_2 = sb("pad_2", [P, 2 * HC * I - HC * TOKENS - 2 * Q * (P + 2)], F32, phase2)
        v16 = sb("v16", [P, 2, 2 * H], BF16, phase2)
        m16 = sb("m16", [P, 2, 2 * H], BF16, phase2)
        v_plus = sb("v_plus", [P, 2, 2 * H], F32, phase2)
        q_raw = sb("q_raw", [P, 2, 2 * H], BF16, phase2)
        q_fp8 = sb("q_fp8", [P, 2, 2 * H], BF16, phase2)
        o_buf = sb("o_buf", [P, 2, 2 * H], F32, phase2)
        phase2.close()

        xt = [t[:] for t in xt_own] + [
            t[:].rearrange("p c t -> p (c t)")[:, 0:Q * (P + 2)].rearrange("p (q n) -> p q n", q=Q)
            for t in (x1_hi, x1_lo)]
        w_max, w_inv, x_max, x_inv, w_scale, w_round, x_scale, x_round, out_scale = (
            small[:, n:n + 1] for n in range(9))
        conv_part = b_buf
        ffn_f = mix[:].rearrange("p g q -> p (g q)")
        ffn_q = agg_b[:, 0:TOKENS // 2].bitcast(BF16)
        w_abs16 = agg_b[:, TOKENS // 2:TOKENS // 2 + H // 2].bitcast(BF16)
        w_m16 = agg_b[:, TOKENS // 2 + H // 2:TOKENS // 2 + H].bitcast(BF16)
        w_plus = agg_b[:, TOKENS // 2 + H:TOKENS // 2 + 2 * H]

        cond_in = sem("cond_in")
        mixw_in = sem("mixw_in")
        x_in = [sem(f"x_in{t}") for t in range(TILES)]
        lr_in = sem("lr_in")
        lrb_in = [sem(f"lrb_in{m}") for m in range(2)]
        scale_in = sem("scale_in")
        down_in = sem("down_in")
        conv_in = sem("conv_in")
        q_in = [sem(f"q_in{n}") for n in range(RING)]
        ffn_in = sem("ffn_in")
        out_done = [sem(f"out_done{n}") for n in range(2)]
        const_set = sem("const_set")
        mix_zero = sem("mix_zero")
        h0_mm, h0_act = sem("h0_mm"), sem("h0_act")
        h1_mm, h1_act = sem("h1_mm"), sem("h1_act")
        logit_mm = sem("logit_mm")
        soft = sem("soft")
        exp_done = sem("exp_done")
        att_tr = sem("att_tr")
        att_ready = sem("att_ready")
        att_rest = sem("att_rest")
        mix_mm = sem("mix_mm")
        mix_ready = sem("mix_ready")
        aggb_mm, aggb_ready = sem("aggb_mm"), sem("aggb_ready")
        ctx_mm, ctx_sum, ctx_full = sem("ctx_mm"), sem("ctx_sum"), sem("ctx_full")
        ctx_hi, ctx_ready = sem("ctx_hi"), sem("ctx_ready")
        q_ready = sem("q_ready")
        scale_ready = sem("scale_ready")
        lra_hi, lra_ready = sem("lra_hi"), sem("lra_ready")
        lrb_hi, lrb_ready = sem("lrb_hi"), sem("lrb_ready")
        down_hi, down_ready = sem("down_hi"), sem("down_ready")
        conv_hi, conv_ready = sem("conv_hi"), sem("conv_ready")
        cond_mm = sem("cond_mm")
        xs_ready = sem("xs_ready")
        x1_hi_ready, x1_lo_ready = sem("x1_hi_ready"), sem("x1_lo_ready")
        p_mm, p_hi_ready, p_lo_ready = sem("p_mm"), sem("p_hi_ready"), sem("p_lo_ready")
        sel_mm, t4_hi_ready, t4_lo_ready = sem("sel_mm"), sem("t4_hi_ready"), sem("t4_lo_ready")
        q_mm, l_mm = sem("q_mm"), sem("l_mm")
        ag_ready, au_ready = sem("ag_ready"), sem("au_ready")
        g_ready, u_ready = sem("g_ready"), sem("u_ready")
        silu_ready, h_ready = sem("silu_ready"), sem("h_ready")
        h_hi_ready, h_lo_ready = sem("h_hi_ready"), sem("h_lo_ready")
        down_mm = sem("down_mm")
        pd_mm, pd_hi_ready, pd_lo_ready = sem("pd_mm"), sem("pd_hi_ready"), sem("pd_lo_ready")
        seld_mm = sem("seld_mm")
        t4d_hi_ready, t4d_lo_ready = sem("t4d_hi_ready"), sem("t4d_lo_ready")
        down_l_mm = sem("down_l_mm")
        yq_ready, y_ready, x2_ready = sem("yq_ready"), sem("y_ready"), sem("x2_ready")
        stage_hi_ready, stage_lo_ready = sem("stage_hi_ready"), sem("stage_lo_ready")
        stored = sem("stored")
        xt_in = [sem(f"xt_in{n}") for n in range(XT)]
        xt_zero = sem("xt_zero")
        conv_mm, part_out, z_ready = sem("conv_mm"), sem("part_out"), sem("z_ready")
        amax_ready = sem("amax_ready")
        wmax, w_diag, w_row_mm, w_steps = sem("wmax"), sem("w_diag"), sem("w_row_mm"), sem("w_steps")
        xmax, x_diag, x_row_mm, x_steps = sem("xmax"), sem("x_diag"), sem("x_row_mm"), sem("x_steps")
        x_scale_ready = sem("x_scale_ready")
        v_ready, m_ready = sem("v_ready"), sem("m_ready")
        w_abs = sem("w_abs")
        wq_step = sem("wq_step")
        wmax_part = sem("wmax_part")
        v_plus_ready = sem("v_plus_ready")
        q_raw_ready, q_own_ready = sem("q_raw_ready"), sem("q_own_ready")
        q_fp8_ready = sem("q_fp8_ready")
        ffn_mm, o_ready = sem("ffn_mm"), sem("o_ready")

        slots = [("gate", ic) if m == 0 else ("up", ic) for ic in range(IC) for m in range(2)]
        slots += [("down", ic) for ic in range(IC)]

        def slot_width(n):
            kind, ic = slots[n]
            return H if kind == "down" else HC * width(ic)

        def slot(n):
            return x_nat[:, GROUPS - RING + n % RING, 0:slot_width(n)].bitcast(I32)

        def slot_dram(n):
            kind, ic = slots[n]
            a = {"gate": gate_q, "up": up_q, "down": down_q}[kind]
            return a[:, H * ic:H * ic + slot_width(n)]

        def slot_weights(n):
            kind, ic = slots[n]
            w = {"gate": gate_w[:], "up": up_w[:], "down": down_w[:].rearrange("p c n -> p (c n)")}[kind]
            return w[:, H * ic:H * ic + slot_width(n)]

        def bank(ic, n):
            return 4 * (ic % 2) + n

        split_buf = [a_buf[:, 1, :], b_buf[:, 1, :], a_buf[:, 0, :], b_buf[:, 0, :]]
        pa = [h_hi[:, IC - 2, :], h_lo[:, IC - 2, :]]
        high_rows, low_rows = (slice(0, 64), slice(64, P)), (slice(64, P), slice(0, 64))
        t4 = [h_hi[:, IC - 1, :], h_lo[:, IC - 1, :]]

        steps = [(sum(STEPS[:n]), k) for n, k in enumerate(STEPS)]

        def by_chunk(ap, k):
            return ap[:, 0:k * H].rearrange("p (c q) -> p c q", c=HC)

        def conv_out(g, part):
            banks = ps[:, 2 * (g % 2):2 * (g % 2) + 2, :].rearrange("p k (b m n) -> p (k b) m n", b=2, m=2)
            return banks[:, :, part, :]

        def plain(ap):
            return ap.bitcast(F32)

        def x_tile(dram, t):
            return dram[t * TILE:(t + 1) * TILE, :].rearrange("(g p) h -> p g h", p=P)

        def expert_bias(engine, b0, b1):
            return engine.tensor_tensor(
                att_bias[:, b0:b1], att_t[:, b0:b1].unsqueeze(2).to_broadcast([EXPERTS, b1 - b0, S]),
                bias_k_sb[:].unsqueeze(1).to_broadcast([EXPERTS, b1 - b0, S]), ALU.mult)

        def spread_mix(copy, q, args):
            for b in range(GB):
                src = ps[q * S:(q + 1) * S, 5, :].rearrange("p (o g b) -> p b g o", g=GROUPS, b=GB)[:, b]
                dst = mix[b * S:(b + 1) * S, :, b * S:(b + 1) * S].rearrange("p g (o q) -> p q g o", q=OB)[:, q]
                last = copy(dst, src, *args)
            return last

        block = ctx.enter_context(nc.Block())

        @block.sync
        def _(sp):
            sp.dma_start(cond_in_sb[:], cond_pack).then_inc(cond_in, 16)
            sp.dma_start(cond_w_sb[:].rearrange("k o p -> k (o p)"), cond_w).then_inc(mixw_in, 16)
            sp.dma_start(bias_k_sb[:], bias_k).then_inc(mixw_in, 16)
            sp.dma_start(ident[:], ident_in).then_inc(lr_in, 16)
            sp.dma_start(stage_sel[:], sel_in).then_inc(lr_in, 16)
            sp.dma_start(stage_lr_a[:].rearrange("p c m r -> p (c m r)"), lr_a).then_inc(lr_in, 16)
            sp.dma_start(x_nat[:, 0:TG, :], x_tile(x, 0)).then_inc(x_in[0], 16)

            def load_slot(n):
                if n >= RING:
                    sp.wait_ge(q_ready, n - RING + 1)
                sp.dma_start(slot(n), slot_dram(n)).then_inc(q_in[n % RING], 16)

            sp.dma_start(stage_gate_b[:], gate_b).then_inc(lrb_in[0], 16)
            for n in range(2):
                load_slot(n)
            sp.dma_start(stage_up_b[:], up_b).then_inc(lrb_in[1], 16)
            for n in range(2, 4):
                load_slot(n)
            sp.dma_start(gate_sc[:], gate_s).then_inc(scale_in, 16)
            sp.dma_start(up_sc[:], up_s).then_inc(scale_in, 16)
            for n in range(4, RING):
                load_slot(n)
            sp.dma_start(down_sb[:], down_s).then_inc(down_in, 16)
            sp.dma_start(stage_down_a[:].rearrange("p c r -> p (c r)"), down_a).then_inc(down_in, 16)
            sp.dma_start(stage_down_b[:], down_b).then_inc(down_in, 16)
            sp.dma_start(stage_conv[:].rearrange("p s n -> p (s n)"), conv_w).then_inc(conv_in, 16)
            sp.dma_start(stage_mask[:], batch_mask).then_inc(conv_in, 16)
            sp.dma_start(stage_side[:], fside).then_inc(conv_in, 16)
            sp.dma_start(stage_ctx_w[:], ctx_w).then_inc(conv_in, 16)
            for n in range(RING, 2 * IC):
                load_slot(n)
            sp.dma_start(x_nat[:, TG:2 * TG, :], x_tile(x, 1)).then_inc(x_in[1], 16)
            for n in range(2 * IC, 3 * IC):
                load_slot(n)
            sp.wait_ge(q_ready, 3 * IC)
            for t in range(2, TILES):
                sp.dma_start(x_nat[:, t * TG:(t + 1) * TG, :], x_tile(x, t)).then_inc(x_in[t], 16)

            def store(g):
                sp.wait_ge(stage_hi_ready, g + 1)
                sp.wait_ge(stage_lo_ready, g + 1)
                sp.dma_start(turned[g].rearrange("m p h -> p m h"), plain(stage[:])).then_inc(stored, 16)

            def load(g):
                sp.wait_ge(stored, 16 * (g + 1))
                if g < XT:
                    sp.wait_ge(q_mm, 2 * TILES * IC)
                    sp.wait_ge(xt_zero, XT)
                else:
                    sp.wait_ge(conv_mm, g - XT + 1)
                sp.dma_start(plain(xt[g % XT][:, :, 1:P + 1]),
                             turned[g].rearrange("m (b c) (k n) -> (c k) (m b) n", b=GB, n=P)
                             ).then_inc(xt_in[g % XT], 16)

            for g in range((TILES - 1) * TG):
                if g == (TILES - 1) * TG - 1:
                    sp.wait_ge(cond_mm, TILES * HC)
                    sp.dma_start(ffn_f, ffn_w).then_inc(ffn_in, 16)
                store(g)
            for g in range(XT):
                load(g)
            for j in range(TG):
                for g in range(CONV_FROM[j] + XT, min(CONV_FROM[j] + CONV_AFTER[j] + XT, GROUPS)):
                    if j == TG - 1 and g == GROUPS - 3:
                        store(GROUPS - 1)
                    load(g)
                if j < TG - 1:
                    store((TILES - 1) * TG + j)
            for n, (g, k) in enumerate(steps):
                sp.wait_ge(o_ready, n + 1)
                sp.dma_start(out[g * P:(g + k) * P, :].rearrange("(k p) h -> p k h", p=P),
                             o_buf[:, n % 2, 0:k * H].rearrange("p (k h) -> p k h", k=k)).then_inc(out_done[n % 2], 16)
            for n in range(2):
                sp.wait_ge(out_done[n], 16 * len(range(n, len(steps), 2)))

        @block.tensor
        def _(pe):
            mm = nc.tensor.matmul

            def keep_clock(n):
                for _ in range(n):
                    mm(ps[:, 7, 0:P], ones[:], ones[:], start=True, stop=True)

            pe.wait_ge(const_set, 1)
            keep_clock(WARM[0])
            pe.wait_ge(cond_in, 16)
            mm(ps[:, 0, 0:B], w0_sb, cond_sb, start=True, stop=True).then_inc(h0_mm, 1)
            keep_clock(WARM[1])
            pe.wait_ge(h0_act, 1)
            mm(ps[:, 1, 0:B], w1_sb, h0[:], start=True, stop=True).then_inc(h1_mm, 1)
            keep_clock(WARM[2])
            pe.wait_ge(h1_act, 1)
            mm(ps[0:B, 2, 0:EXPERTS], h1[:], w2_sb, start=True, stop=True).then_inc(logit_mm, 1)
            keep_clock(WARM[3])
            pe.wait_ge(soft, 4)
            pe.wait_ge(lr_in, 3 * 16)
            nc.tensor.transpose(ps[0:EXPERTS, 3, 0:B], att[:], ident[0:B, 0:B]).then_inc(att_tr, 1)
            pe.wait_ge(att_ready, 1)
            pe.wait_ge(mixw_in, 2 * 16)
            for o in range(S // OB):
                last = mm(ps[:, 5, o * B:(o + 1) * B], cond_w_sb[:, o, :], att_t[:], start=True, stop=True)
            last.then_inc(mix_mm, 1)

            def mixed_bias(t):
                mm(ps[:, BIAS_BANK[t], :], ones[0:EXPERTS, :],
                   att_bias[:].rearrange("k b s -> k (b s)")[:, t * TILE:(t + 1) * TILE],
                   start=True, stop=True).then_inc(aggb_mm, 1)

            pe.wait_ge(att_ready, 2)
            mixed_bias(0)

            def condition(t):
                pe.wait_ge(x_in[t], 16)
                for c in range(HC):
                    for g in range(t * TG, (t + 1) * TG):
                        last = mm(ps[:, c, (g % TG) * P:(g % TG + 1) * P], x_nat[:, g, c * P:(c + 1) * P],
                                  mix[:, g, :], start=True, stop=True)
                    last.then_inc(cond_mm, 1)

            def down_repeat(t):
                pe.wait_ge(pd_hi_ready, t + 1)
                pe.wait_ge(pd_lo_ready, t + 1)
                mm(ps[:, 7, :], sel[:], pd[:], start=True, stop=True).then_inc(seld_mm, 1)

            def down_low_rank(t, j):
                if j == 0:
                    pe.wait_ge(t4d_hi_ready, t + 1)
                    pe.wait_ge(t4d_lo_ready, t + 1)
                mm(ps[:, 6 + j % 2, :], t4d[:, j * P:(j + 1) * P], down_b4[:],
                   start=True, stop=True).then_inc(down_l_mm, 1)

            def down(t, j):
                if j == 0:
                    pe.wait_ge(u_ready, t * IC + IC - 1)
                    if t == 0:
                        pe.wait_ge(down_ready, 1)
                if j >= 2:
                    pe.wait_ge(y_ready, t * TG + j - 1)
                for ic in range(IC):
                    k = width(ic)
                    if j == 0:
                        pe.wait_ge(h_lo_ready, t * IC + ic + 1)
                        if t == 0:
                            pe.wait_ge(q_ready, 2 * IC + ic + 1)
                    if j == 1 and ic == 3:
                        down_repeat(t)
                    if j == 1 and ic == 8:
                        down_low_rank(t, 0)
                    for part in (h_hi, h_lo):
                        first, end = ic == 0 and part is h_hi, ic == IC - 1 and part is h_lo
                        if j == 0:
                            low = mm(ps[0:2 * R, 6, :], down_a_w[0:k, ic].rearrange("p m r -> p (m r)"),
                                     part[0:k, ic, :], start=first, stop=end)
                        last = mm(ps[:, 4 + j % 2, :], part[0:k, ic, j * P:(j + 1) * P], down_w[0:k, ic, :],
                                  start=first, stop=end)
                if j == 0:
                    low.then_inc(pd_mm, 1)
                last.then_inc(down_mm, 1)
                if j > 0:
                    down_low_rank(t, j)

            def quantised(t, ic, m):
                if t == 0:
                    pe.wait_ge(q_ready, 2 * ic + m + 1)
                w = (gate_w, up_w)[m]
                k = width(ic)
                for c in range(HC):
                    for part in (x1_hi, x1_lo):
                        last = mm(ps[0:k, bank(ic, 2 * m), :], w[:, H * ic + c * k:H * ic + (c + 1) * k],
                                  part[:, c, :], start=c == 0 and part is x1_hi, stop=c == HC - 1 and part is x1_lo)
                last.then_inc(q_mm, 1)

            def low_rank(t, ic, m):
                w = (gate_b4, up_b4)[m]
                mm(ps[0:width(ic), bank(ic, 2 * m + 1), :], w[:, ic * P:ic * P + width(ic)], t4[m],
                   start=True, stop=True).then_inc(l_mm, 1)

            def spread(diagonal, to, mm_sem):
                pe.wait_ge(diagonal, 1)
                mm(ps[:, to, 0:P], ones[:], diag[:], start=True, stop=True).then_inc(mm_sem, 1)

            def convolve(g):
                pe.wait_ge(xt_in[g % XT], 16 * (g // XT + 1))
                if g == 0:
                    pe.wait_ge(conv_ready, 1)
                    pe.wait_ge(ctx_ready, 2)
                    pe.wait_ge(u_ready, TILES * IC)
                if g >= 2:
                    pe.wait_ge(z_ready, g - 1)
                for b in range(GB):
                    bank_out = ps[:, 2 * (g % 2) + b // 2, :].rearrange("p (b n) -> p b n", b=2)
                    for k in range(SHIFTS):
                        for m in range(2):
                            mm(bank_out[:, b % 2, :], xt[g % XT][:, m * GB + b, k:k + P],
                               conv_wt[:, k].rearrange("p m n -> p (m n)"),
                               start=b % 2 == 0 and k == 0 and m == 0, stop=False)
                    if b % 2 == 1:
                        last = mm(bank_out[:, :, 0:P].rearrange("p b (f o) -> p b f o", f=PHASES),
                                  ctx_pick[:, g:g + 1].to_broadcast([P, P]),
                                  ctx_rhs[:, b - 1:b + 1].unsqueeze(2).to_broadcast([P, 2, PHASES, S]),
                                  start=False, stop=True)
                last.then_inc(conv_mm, 1)

            keep_clock(WARM[4])
            pe.wait_ge(mix_ready, 2)
            condition(0)

            def context():
                pe.wait_ge(conv_in, 4 * 16)
                pe.wait_ge(aggb_ready, 1)
                for m in range(2):
                    last = mm(ps[m * B:(m + 1) * B, 4, 0:S], cond_sb, stage_ctx_w[:], start=True, stop=True)
                last.then_inc(ctx_mm, 1)
                pe.wait_ge(aggb_ready, 3)

            for t in range(TILES):
                if t == 0:
                    pe.wait_ge(lra_ready, 1)
                for c in range(HC):
                    if t == 0 and c > 0:
                        if c == 1:
                            pe.wait_ge(att_rest, 1)
                        mixed_bias(c)
                    pe.wait_ge(x1_hi_ready, t * HC + c + 1)
                    pe.wait_ge(x1_lo_ready, t * HC + c + 1)
                    for part in (x1_hi, x1_lo):
                        last = mm(ps[:, bank(0, 1), :], lr_a_w[:, c].rearrange("p m v r -> p (m v r)"),
                                  part[:, c, :], start=c == 0 and part is x1_hi,
                                  stop=c == HC - 1 and part is x1_lo)
                last.then_inc(p_mm, 1)
                quantised(t, 0, 0)
                quantised(t, 0, 1)
                if t == 0:
                    context()
                pe.wait_ge(p_hi_ready, 2 * (t + 1))
                pe.wait_ge(p_lo_ready, 2 * (t + 1))
                if t > 0:
                    pe.wait_ge(y_ready, t * TG)
                for m in range(2):
                    mm(ps[:, bank(1, 2 * m + 1), :], sel[:], pa[m], start=True, stop=True).then_inc(sel_mm, 1)
                if t == 0:
                    pe.wait_ge(lrb_ready, 2)
                for m in range(2):
                    if t == 0 and m == 0:
                        pe.wait_ge(ctx_sum, 1)
                    if t == 0 and m == 1:
                        pe.wait_ge(aggb_ready, TILES)
                    quantised(t, 1, m)
                    pe.wait_ge(t4_hi_ready, 2 * t + m + 1)
                    pe.wait_ge(t4_lo_ready, 2 * t + m + 1)
                    low_rank(t, 0, m)
                low_rank(t, 1, 0)
                low_rank(t, 1, 1)
                for ic in range(2, IC):
                    for m in range(2):
                        pe.wait_ge((g_ready, u_ready)[m], t * IC + ic - 1)
                        if t == TILES - 1 and ic == W_SPREAD and m == 0:
                            spread(w_diag, bank(ic, 1), w_row_mm)
                        quantised(t, ic, m)
                        if t == TILES - 1 and ic == W_SPREAD and m == 0:
                            pe.wait_ge(w_steps, 1)
                        low_rank(t, ic, m)
                for j in range(TG):
                    down(t, j)
                    if t + 1 < TILES and j == TG - 2:
                        condition(t + 1)
                    if t == TILES - 1:
                        for n in range(CONV_AFTER[j]):
                            convolve(CONV_FROM[j] + n)
            spread(x_diag, 6, x_row_mm)
            pe.wait_ge(wq_step, W_STEPS * HC)
            for n, (g, k) in enumerate(steps):
                pe.wait_ge(q_fp8_ready, n + 1)
                if n >= 2:
                    pe.wait_ge(o_ready, n - 1)
                for j in range(k):
                    for c in range(HC):
                        last = mm(ps[:, 2 * (n % 2) + j, :], by_chunk(q_fp8[:, n % 2], k)[:, c, j * P:(j + 1) * P],
                                  ffn_q[:, c * H:(c + 1) * H], start=c == 0, stop=c == HC - 1)
                last.then_inc(ffn_mm, 1)

        @block.scalar
        def _(act):
            copy, activation = ACT.Copy, nc.scalar.activation
            act.wait_ge(cond_in, 16)
            act.wait_ge(h0_mm, 1)
            activation(h0[:], ps[:, 0, 0:B], ACT.Gelu, bias=b0_sb).then_inc(h0_act, 1)
            act.wait_ge(h1_mm, 1)
            activation(h1[:], ps[:, 1, 0:B], ACT.Gelu, bias=b1_sb).then_inc(h1_act, 1)
            act.wait_ge(soft, 2)
            activation(probs[:], logits[:], ACT.Exp, bias=stat[:, 0:1], accum_out=stat[:, 1:2]).then_inc(exp_done, 1)
            act.wait_ge(lr_in, 3 * 16)
            activation(sel[:], stage_sel[:], copy)
            activation(lr_a_w[:, :, :, 0, :], stage_lr_a[:], copy).then_inc(lra_hi, 1)
            act.wait_ge(mix_mm, 1)
            act.wait_ge(mix_zero, 1)
            for q in range(2, OB):
                last = spread_mix(activation, q, (copy,))
            last.then_inc(mix_ready, 1)

            def split_mixed(t):
                for c in range(HC):
                    act.wait_ge(xs_ready, t * HC + c + 1)
                    activation(x1_hi[:, c, :], split_buf[c], copy).then_inc(x1_hi_ready, 1)

            def keep_bias(t):
                act.wait_ge(aggb_mm, t + 1)
                activation(agg_b[:, t * TILE:(t + 1) * TILE], ps[:, BIAS_BANK[t], :], copy).then_inc(aggb_ready, 1)

            def x_a_high(t):
                act.wait_ge(p_mm, t + 1)
                for m, rows in enumerate(high_rows):
                    activation(pa[m][rows], ps[rows, bank(0, 1), :], copy, scale=LR_SCALE).then_inc(p_hi_ready, 1)

            keep_bias(0)
            act.wait_ge(lrb_in[0], 16)
            activation(gate_b4[:], stage_gate_b[:], copy).then_inc(lrb_hi, 1)
            split_mixed(0)
            act.wait_ge(lrb_in[1], 16)
            activation(up_b4[:], stage_up_b[:], copy).then_inc(lrb_hi, 1)
            x_a_high(0)
            act.wait_ge(down_in, 3 * 16)
            activation(down_a_w[:, :, 0, :], stage_down_a[:], copy).then_inc(down_hi, 1)
            activation(down_b4[:], stage_down_b[:], copy).then_inc(down_hi, 1)
            for t in range(1, TILES):
                keep_bias(t)

            def repeated_high(t):
                for m in range(2):
                    act.wait_ge(sel_mm, 2 * t + m + 1)
                    activation(t4[m], ps[:, bank(1, 2 * m + 1), :], copy).then_inc(t4_hi_ready, 1)

            def convolution_high():
                act.wait_ge(conv_in, 4 * 16)
                activation(conv_wt[:, :, 0, :], stage_conv[:], copy).then_inc(conv_hi, 1)
                activation(ctx_pick[:], stage_mask[:, GB:], copy).then_inc(ctx_ready, 1)
                act.wait_ge(ctx_full, 1)
                activation(ctx_rhs[:].rearrange("p b o -> p (b o)"), y_buf[:, 1, 0:P], copy).then_inc(ctx_hi, 1)

            def down_parts_high(t):
                act.wait_ge(pd_mm, t + 1)
                activation(pd[0:2 * R, :], ps[0:2 * R, 6, :], copy, scale=LR_SCALE).then_inc(pd_hi_ready, 1)

            def down_high(t):
                act.wait_ge(seld_mm, t + 1)
                activation(t4d[:], ps[:, 7, :], copy).then_inc(t4d_hi_ready, 1)

            def h_high(t, ic):
                n = t * IC + ic
                act.wait_ge(h_ready, n + 1)
                k = width(ic)
                activation(h_hi[0:k, ic, :], a_buf[0:k, ic % 2, :], copy).then_inc(h_hi_ready, 1)

            def stage_high(g):
                act.wait_ge(x2_ready, g + 1)
                if g > 0:
                    act.wait_ge(stored, 16 * g)
                activation(stage[:, 0, :], x_nat[:, g, :], copy).then_inc(stage_hi_ready, 1)

            def conv_low(g):
                act.wait_ge(conv_mm, g + 1)
                if g == 0:
                    act.wait_ge(h_ready, TILES * IC)
                if g >= 2:
                    act.wait_ge(z_ready, g - 1)
                activation(conv_part[:, g % 2, :].rearrange("p (b n) -> p b n", b=GB), conv_out(g, 1),
                           copy).then_inc(part_out, 1)

            for t in range(TILES):
                if t > 0:
                    x_a_high(t)
                else:
                    act.wait_ge(scale_ready, 2)
                for ic in range(IC):
                    n = t * IC + ic
                    k = width(ic)
                    if n == 0:
                        repeated_high(t)
                    act.wait_ge(q_mm, 2 * n + 1)
                    if ic >= 2:
                        act.wait_ge(h_lo_ready, n - 1)
                    activation(a_buf[0:k, ic % 2, :], ps[0:k, bank(ic, 0), :], copy,
                               scale=gate_sc[0:k, ic:ic + 1]).then_inc(ag_ready, 1)
                    act.wait_ge(q_mm, 2 * n + 2)
                    activation(b_buf[0:k, ic % 2, :], ps[0:k, bank(ic, 2), :], copy,
                               scale=up_sc[0:k, ic:ic + 1]).then_inc(au_ready, 1)
                    if ic == 0 and t > 0:
                        repeated_high(t)
                    if ic >= 1:
                        h_high(t, ic - 1)
                    if ic == 3 and t > 0:
                        stage_high(t * TG - 1)
                    if ic == 1 and t == 0:
                        convolution_high()
                    act.wait_ge(g_ready, n + 1)
                    activation(a_buf[0:k, ic % 2, :], a_buf[0:k, ic % 2, :], ACT.Silu).then_inc(silu_ready, 1)
                    if t == TILES - 1 and W_SPREAD <= ic < W_SPREAD + HC:
                        c = ic - W_SPREAD
                        if c == 0:
                            act.wait_ge(w_steps, 5)
                        else:
                            act.wait_ge(wq_step, (c - 1) * W_STEPS + 1)
                        activation(w_abs16, ffn_f[:, c * H:(c + 1) * H], ACT.Abs,
                                   scale=w_round).then_inc(w_abs, 1)
                h_high(t, IC - 1)
                down_parts_high(t)
                for j in range(TG):
                    if j == 0 and t < TILES - 1:
                        down_high(t)
                    if j == 2 and t < TILES - 1:
                        split_mixed(t + 1)
                    if j < TG - 1 and t < TILES - 1:
                        stage_high(t * TG + j)
                    if t == TILES - 1:
                        first, end = CONV_FROM[j], CONV_FROM[j] + CONV_AFTER[j]
                        before = (CONV_AFTER[0], 1, 1, 0)[j]
                        for g in range(first, first + before):
                            conv_low(g)
                        if j == 0:
                            down_high(t)
                        stage_high(t * TG + j)
                        for g in range(first + before, end):
                            conv_low(g)
            act.wait_ge(x_scale_ready, 1)
            for n, (g, k) in enumerate(steps):
                if n >= 2:
                    act.wait_ge(m_ready, n - 1)
                activation(by_chunk(v16[:, n % 2], k), t_t[:, :, g * P:(g + k) * P], ACT.Abs,
                           scale=x_round).then_inc(v_ready, 1)

        @block.gpsimd
        def _(pool):
            nc.gpsimd.memset(mix[:], 0.0).then_inc(mix_zero, 1)
            pool.wait_ge(att_ready, 1)
            pool.wait_ge(mixw_in, 2 * 16)
            expert_bias(nc.gpsimd, TILE // S, B).then_inc(att_rest, 1)
            for m, (w, st) in enumerate(((gate_b4, stage_gate_b), (up_b4, stage_up_b))):
                pool.wait_ge(lrb_hi, m + 1)
                for q in (1, 3):
                    rows = slice(q * S, (q + 1) * S)
                    last = nc.gpsimd.tensor_tensor(w[rows, :], st[rows, :], plain(w[rows, :]), ALU.subtract)
                last.then_inc(lrb_ready, 1)

            def stage_low(g):
                pool.wait_ge(stage_hi_ready, g + 1)
                nc.gpsimd.tensor_tensor(stage[:, 1, :], x_nat[:, g, :], plain(stage[:, 0, :]),
                                        ALU.subtract).then_inc(stage_lo_ready, 1)

            for t in range(TILES):
                for ic in range(IC):
                    n = t * IC + ic
                    k = width(ic)
                    pool.wait_ge(h_hi_ready, n + 1)
                    nc.gpsimd.tensor_tensor(h_lo[0:k, ic, :], a_buf[0:k, ic % 2, :], plain(h_hi[0:k, ic, :]),
                                            ALU.subtract).then_inc(h_lo_ready, 1)
                    if ic == 3 and t > 0:
                        stage_low(t * TG - 1)
                for j in range(TG if t + 1 < TILES else TG - 1):
                    n = t * TG + j
                    pool.wait_ge(y_ready, n + 1)
                    nc.gpsimd.tensor_tensor(x_nat[:, n, :], y_buf[:, j % 2, :], x_nat[:, n, :],
                                            ALU.add).then_inc(x2_ready, 1)
                    if j < TG - 1:
                        stage_low(n)
            for n, (g, k) in enumerate(steps):
                if k == 1:
                    continue
                pool.wait_ge(v_plus_ready, n + 1)
                if n >= 2:
                    pool.wait_ge(q_fp8_ready, n - 1)
                nc.gpsimd.tensor_tensor(q_raw[:, n % 2, 0:k * H], v_plus[:, n % 2, 0:k * H], m16[:, n % 2, 0:k * H],
                                        ALU.subtract).then_inc(q_raw_ready, 1)

        @block.vector
        def _(dve):
            v = nc.vector
            v.memset(ones[:], 1.0).then_inc(const_set, 1)
            dve.wait_ge(cond_in, 16)
            dve.wait_ge(logit_mm, 1)
            v.tensor_tensor(logits[:], ps[0:B, 2, 0:EXPERTS], b2_sb, ALU.add).then_inc(soft, 1)
            dve.wait_ge(soft, 1)
            v.tensor_reduce(stat[:, 0:1], logits[:], AX_X, ALU.max, negate=True).then_inc(soft, 1)
            dve.wait_ge(exp_done, 1)
            v.reciprocal(stat[:, 2:3], stat[:, 1:2]).then_inc(soft, 1)
            dve.wait_ge(soft, 3)
            v.tensor_scalar(att[:], probs[:], stat[:, 2:3], None, ALU.mult).then_inc(soft, 1)
            dve.wait_ge(att_tr, 1)
            v.tensor_copy(att_t[:], ps[0:EXPERTS, 3, 0:B]).then_inc(att_ready, 1)
            dve.wait_ge(att_ready, 1)
            dve.wait_ge(mixw_in, 2 * 16)

            expert_bias(v, 0, TILE // S).then_inc(att_ready, 1)
            dve.wait_ge(mix_mm, 1)
            dve.wait_ge(mix_zero, 1)
            for q in range(2):
                last = spread_mix(v.tensor_copy, q, ())
            last.then_inc(mix_ready, 1)

            def convert(n):
                dve.wait_ge(q_in[n % RING], 16 * (n // RING + 1))
                v.tensor_scalar(slot_weights(n), slot(n), Q_ZERO, None, ALU.subtract).then_inc(q_ready, 1)

            def split_mixed(t):
                for c in range(HC):
                    dve.wait_ge(cond_mm, t * HC + c + 1)
                    v.tensor_tensor(split_buf[c], ps[:, c, :], agg_b[:, t * TILE:(t + 1) * TILE],
                                    ALU.add).then_inc(xs_ready, 1)
                    if c > 0:
                        split_low(t, c - 1)
                split_low(t, HC - 1)

            def split_low(t, c):
                dve.wait_ge(x1_hi_ready, t * HC + c + 1)
                v.tensor_tensor(x1_lo[:, c, :], split_buf[c], plain(x1_hi[:, c, :]),
                                ALU.subtract).then_inc(x1_lo_ready, 1)

            def x_a_low(t):
                for m in range(2):
                    dve.wait_ge(p_hi_ready, 2 * t + m + 1)
                    v.scalar_tensor_tensor(pa[m][low_rows[m]], ps[high_rows[m], bank(0, 1), :], LR_SCALE,
                                           plain(pa[m][high_rows[m]]), ALU.mult, ALU.subtract).then_inc(p_lo_ready, 1)

            dve.wait_ge(lra_hi, 1)
            v.tensor_tensor(lr_a_w[:, :, :, 1, :], stage_lr_a[:], plain(lr_a_w[:, :, :, 0, :]),
                            ALU.subtract).then_inc(lra_ready, 1)
            convert(0)
            convert(1)
            dve.wait_ge(aggb_ready, 1)
            split_mixed(0)
            dve.wait_ge(scale_in, 2 * 16)
            v.tensor_scalar(gate_sc[:], gate_sc[:], Q_STEP, None, ALU.mult).then_inc(scale_ready, 1)
            v.tensor_scalar(up_sc[:], up_sc[:], Q_STEP, None, ALU.mult).then_inc(scale_ready, 1)
            x_a_low(0)
            convert(2)
            convert(3)
            dve.wait_ge(down_hi, 2)
            v.tensor_tensor(down_a_w[:, :, 1, :], stage_down_a[:], plain(down_a_w[:, :, 0, :]), ALU.subtract)
            for q in (1, 3):
                rows = slice(q * S, (q + 1) * S)
                v.tensor_tensor(down_b4[rows, :], stage_down_b[rows, :], plain(down_b4[rows, :]), ALU.subtract)
            dve.wait_ge(down_in, 3 * 16)
            v.tensor_scalar(down_sb[:], down_sb[:], Q_STEP, None, ALU.mult).then_inc(down_ready, 1)
            dve.wait_ge(conv_in, 4 * 16)
            dve.wait_ge(ctx_mm, 1)
            v.tensor_tensor(y_buf[:, 0, 0:S], ps[:, 4, 0:S], stage_side[:], ALU.add).then_inc(ctx_sum, 1)
            dve.wait_ge(ctx_sum, 1)
            v.tensor_tensor(y_buf[:, 1, 0:P].rearrange("p (b o) -> p b o", b=GB),
                            y_buf[:, 0, 0:S].unsqueeze(1).to_broadcast([P, GB, S]),
                            stage_mask[:, 0:GB].unsqueeze(2).to_broadcast([P, GB, S]), ALU.mult).then_inc(ctx_full, 1)

            def convolution_low():
                dve.wait_ge(conv_hi, 1)
                v.tensor_tensor(conv_wt[:, :, 1, :], stage_conv[:], plain(conv_wt[:, :, 0, :]),
                                ALU.subtract).then_inc(conv_ready, 1)
                dve.wait_ge(ctx_hi, 1)
                low = ctx_rhs[B:P].rearrange("p b o -> p (b o)")
                v.tensor_tensor(low, y_buf[B:P, 1, 0:P], plain(low), ALU.subtract).then_inc(ctx_ready, 1)

            def down_scaled(t, j):
                n = t * TG + j
                dve.wait_ge(down_mm, n + 1)
                if n >= 2:
                    dve.wait_ge(x2_ready, n - 1)
                v.tensor_tensor(y_buf[:, j % 2, :], ps[:, 4 + j % 2, :], down_sb[:], ALU.mult).then_inc(yq_ready, 1)

            def down_parts_low(t):
                dve.wait_ge(pd_hi_ready, t + 1)
                v.scalar_tensor_tensor(pd[2 * R:P, :], ps[0:2 * R, 6, :], LR_SCALE, plain(pd[0:2 * R, :]), ALU.mult,
                                       ALU.subtract).then_inc(pd_lo_ready, 1)

            def down_low(t):
                dve.wait_ge(t4d_hi_ready, t + 1)
                v.tensor_tensor(t4d[64:P, :], ps[64:P, 7, :], plain(t4d[64:P, :]), ALU.subtract).then_inc(
                    t4d_lo_ready, 1)

            def down_sum(t, j):
                n = t * TG + j
                dve.wait_ge(down_l_mm, n + 1)
                dve.wait_ge(yq_ready, n + 1)
                v.tensor_tensor(y_buf[:, j % 2, :], ps[:, 6 + j % 2, :], y_buf[:, j % 2, :],
                                ALU.add).then_inc(y_ready, 1)

            def diagonal(col, largest, done):
                dve.wait_ge(largest, 1)
                v.tensor_scalar(diag[:], ident[:], amax[:, col:col + 1], None, ALU.mult).then_inc(done, 1)

            def scale_from(row_mm, at, largest, inverse, steps_done):
                dve.wait_ge(row_mm, 1)
                v.tensor_reduce(largest, ps[:, at, 0:P], AX_X, ALU.max).then_inc(steps_done, 1)
                dve.wait_ge(steps_done, 1)
                v.tensor_scalar(largest, largest, AMAX_MIN, None, ALU.max).then_inc(steps_done, 1)
                dve.wait_ge(steps_done, 2)
                v.reciprocal(inverse, largest).then_inc(steps_done, 1)
                dve.wait_ge(steps_done, 3)

            def weight_max(c):
                dve.wait_ge(ffn_in, 16)
                v.tensor_reduce(amax[:, WMAX + c:WMAX + c + 1], ffn_f[:, c * H:(c + 1) * H], AX_X, ALU.max,
                                apply_absolute_value=True).then_inc(wmax_part, 1)

            def weight_largest():
                dve.wait_ge(wmax_part, HC)
                v.tensor_reduce(amax[:, XMAX + 1:XMAX + 2], amax[:, WMAX:WMAX + HC], AX_X, ALU.max).then_inc(wmax, 1)
                diagonal(XMAX + 1, wmax, w_diag)

            def weight_scale():
                scale_from(w_row_mm, bank(W_SPREAD, 1), w_max, w_inv, w_steps)
                v.tensor_scalar(w_scale, w_inv, FP8_MAX, None, ALU.mult).then_inc(w_steps, 1)
                v.tensor_scalar(w_round, w_inv, FP8_MAX, ROUND_SCALE, ALU.mult,
                                ALU.mult).then_inc(w_steps, 1)
                dve.wait_ge(w_steps, 5)

            def round_weight(n):
                c = n // W_STEPS
                w = ffn_f[:, c * H:(c + 1) * H]
                if n > 0:
                    dve.wait_ge(wq_step, n)
                if n % W_STEPS == 0:
                    dve.wait_ge(w_abs, c + 1)
                    v.tensor_scalar(w_m16, w_abs16, ROUND_MIN, None, ALU.max).then_inc(wq_step, 1)
                elif n % W_STEPS == 1:
                    v.scalar_tensor_tensor(w_plus, w, w_scale, w_m16, ALU.mult, ALU.add).then_inc(wq_step, 1)
                elif n % W_STEPS == 2:
                    v.tensor_tensor(w_m16, w_plus, w_m16, ALU.subtract).then_inc(wq_step, 1)
                else:
                    v.tensor_scalar(ffn_q[:, c * H:(c + 1) * H], w_m16, FP8_MAX, -FP8_MAX, ALU.min,
                                    ALU.max).then_inc(wq_step, 1)

            def conv_sum(g):
                dve.wait_ge(part_out, g + 1)
                if g == 0:
                    dve.wait_ge(q_mm, 2 * TILES * IC)
                v.tensor_tensor(t_t[:, :, g * P:(g + 1) * P].rearrange("p f (b o) -> p b f o", b=GB),
                                conv_out(g, 0).rearrange("p b (f o) -> p b f o", f=PHASES),
                                conv_part[:, g % 2, :].rearrange("p (b f o) -> p b f o", b=GB, f=PHASES),
                                ALU.add).then_inc(z_ready, 1)
                dve.wait_ge(z_ready, g + 1)
                v.tensor_reduce(amax[:, PHASES * g:PHASES * (g + 1)], t_t[:, :, g * P:(g + 1) * P], AX_X, ALU.max,
                                apply_absolute_value=True).then_inc(amax_ready, 1)

            for t in range(TILES):
                if t > 0:
                    x_a_low(t)
                for m in range(2):
                    dve.wait_ge(t4_hi_ready, 2 * t + m + 1)
                    v.tensor_tensor(t4[m][64:P], ps[64:P, bank(1, 2 * m + 1), :], plain(t4[m][64:P]),
                                    ALU.subtract).then_inc(t4_lo_ready, 1)
                for ic in range(IC):
                    n = t * IC + ic
                    k = width(ic)
                    a, b = a_buf[0:k, ic % 2, :], b_buf[0:k, ic % 2, :]
                    if t == 0 and ic == 2:
                        convolution_low()
                    if t == 0:
                        for later in range(2 * ic + 4, min(2 * ic + 6, 2 * IC)):
                            convert(later)
                        if 2 * ic + 4 >= 2 * IC:
                            for later in range(2 * IC + 2 * (ic - IC + 2), 2 * IC + 2 * (ic - IC + 3)):
                                convert(later)
                    dve.wait_ge(ag_ready, n + 1)
                    dve.wait_ge(l_mm, 2 * n + 1)
                    v.tensor_tensor(a, ps[0:k, bank(ic, 1), :], a, ALU.add).then_inc(g_ready, 1)
                    dve.wait_ge(au_ready, n + 1)
                    dve.wait_ge(l_mm, 2 * n + 2)
                    v.tensor_tensor(b, ps[0:k, bank(ic, 3), :], b, ALU.add).then_inc(u_ready, 1)
                    dve.wait_ge(silu_ready, n + 1)
                    dve.wait_ge(u_ready, n + 1)
                    v.tensor_tensor(a, a, b, ALU.mult).then_inc(h_ready, 1)
                    if t == TILES - 1:
                        if ic in (1, 2):
                            weight_max(2 * ic - 2)
                            weight_max(2 * ic - 1)
                        if ic == 3:
                            weight_largest()
                        if ic == W_SPREAD - 1:
                            weight_scale()
                        if ic >= W_SPREAD:
                            first = W_EACH * (ic - W_SPREAD)
                            for n in range(first, min(first + W_EACH, W_STEPS * HC)):
                                round_weight(n)
                if t == 0:
                    for later in range(2 * IC + 4, 3 * IC):
                        convert(later)
                if t == TILES - 1:
                    dve.wait_ge(q_mm, 2 * TILES * IC)
                    for n in range(XT):
                        for at in (0, P + 1):
                            last = v.memset(plain(xt[n][:, :, at:at + 1]), 0.0)
                        last.then_inc(xt_zero, 1)
                down_parts_low(t)
                for j in range(TG):
                    down_scaled(t, j)
                    if j == 0:
                        if t == TILES - 1:
                            for n in range(CONV_AFTER[0]):
                                conv_sum(n)
                        down_low(t)
                    down_sum(t, j)
                    if j == 2 and t + 1 < TILES:
                        split_mixed(t + 1)
                    if t == TILES - 1 and 0 < j < TG - 1:
                        for n in range(CONV_AFTER[j]):
                            conv_sum(CONV_FROM[j] + n)
            n = GROUPS - 1
            dve.wait_ge(y_ready, n + 1)
            v.tensor_tensor(x_nat[:, n, :], y_buf[:, n % 2, :], x_nat[:, n, :], ALU.add).then_inc(x2_ready, 1)
            dve.wait_ge(stage_hi_ready, n + 1)
            v.tensor_tensor(stage[:, 1, :], x_nat[:, n, :], plain(stage[:, 0, :]),
                            ALU.subtract).then_inc(stage_lo_ready, 1)
            for g in range(CONV_FROM[-1], GROUPS):
                conv_sum(g)
            dve.wait_ge(amax_ready, GROUPS)
            v.tensor_reduce(amax[:, XMAX:XMAX + 1], amax[:, 0:XMAX], AX_X, ALU.max).then_inc(xmax, 1)
            diagonal(XMAX, xmax, x_diag)
            scale_from(x_row_mm, 6, x_max, x_inv, x_steps)
            v.tensor_scalar(x_round, x_inv, FP8_MAX, ROUND_SCALE, ALU.mult,
                            ALU.mult).then_inc(x_scale_ready, 1)
            v.tensor_scalar(x_scale, x_inv, FP8_MAX, None, ALU.mult).then_inc(x_scale_ready, 1)
            v.tensor_scalar(out_scale, x_max, 1.0 / FP8_MAX, None, ALU.mult).then_inc(x_scale_ready, 1)
            dve.wait_ge(x_scale_ready, 3)
            v.tensor_scalar(out_scale, out_scale, w_max, 1.0 / FP8_MAX, ALU.mult,
                            ALU.mult).then_inc(x_scale_ready, 1)

            def subtract(n, k):
                dve.wait_ge(v_plus_ready, n + 1)
                v.tensor_tensor(q_raw[:, n % 2, 0:k * H], v_plus[:, n % 2, 0:k * H], m16[:, n % 2, 0:k * H],
                                ALU.subtract).then_inc(q_own_ready, 1)

            def wait_subtracted(n):
                own = steps[n][1] == 1
                dve.wait_ge(q_own_ready if own else q_raw_ready,
                            sum((k == 1) == own for _, k in steps[:n + 1]))

            def clip(n, k):
                wait_subtracted(n)
                if n >= 2:
                    dve.wait_ge(ffn_mm, n - 1)
                v.tensor_scalar(q_fp8[:, n % 2, 0:k * H], q_raw[:, n % 2, 0:k * H], FP8_MAX, -FP8_MAX,
                                ALU.min, ALU.max).then_inc(q_fp8_ready, 1)

            def output(n, g, k):
                if n == 0:
                    dve.wait_ge(x_scale_ready, 4)
                dve.wait_ge(ffn_mm, n + 1)
                if n >= 2:
                    dve.wait_ge(out_done[n % 2], 16 * (n // 2))
                banks = ps[:, 2 * (n % 2):2 * (n % 2) + k, :].rearrange("p k h -> p (k h)")
                v.scalar_tensor_tensor(o_buf[:, n % 2, 0:k * H], banks, out_scale,
                                       x_nat[:, g:g + k, :].rearrange("p k h -> p (k h)"),
                                       ALU.mult, ALU.add).then_inc(o_ready, 1)

            for n, (g, k) in enumerate(steps):
                v_step, m = v16[:, n % 2, 0:k * H], m16[:, n % 2, 0:k * H]
                dve.wait_ge(v_ready, n + 1)
                if n >= 2:
                    wait_subtracted(n - 2)
                v.tensor_scalar(m, v_step, ROUND_MIN, None, ALU.max).then_inc(m_ready, 1)
                dve.wait_ge(m_ready, n + 1)
                v.scalar_tensor_tensor(by_chunk(v_plus[:, n % 2], k), t_t[:, :, g * P:(g + k) * P], x_scale,
                                       by_chunk(m16[:, n % 2], k), ALU.mult, ALU.add).then_inc(v_plus_ready, 1)
                if k == 1:
                    subtract(n, k)
                    if n == 0:
                        clip(n, k)
                if n >= 2:
                    clip(n - 1, steps[n - 1][1])
                if n >= 2:
                    output(n - 2, *steps[n - 2])
            n = len(steps) - 1
            clip(n, steps[n][1])
            output(n - 1, *steps[n - 1])
            output(n, *steps[n])


def kernel(x, cond_128, fside_S_0, L0_cond_W0, L0_cond_b0, L0_cond_W1, L0_cond_b1, L0_cond_W2, L0_cond_b2,
           L0_cond_weight, L0_cond_bias_k, L0_ffn_gate_q, L0_ffn_gate_scale, L0_ffn_gate_A, L0_ffn_gate_B,
           L0_ffn_up_q, L0_ffn_up_scale, L0_ffn_up_A, L0_ffn_up_B, L0_ffn_down_q, L0_ffn_down_scale,
           L0_ffn_down_A, L0_ffn_down_B, L1_cond_weight, L1_cond_c_weight, L1_ffn_weight):
    import numpy as np
    import concourse.bacc as bacc
    from concourse.bass_utils import run_bass_kernel_spmd

    a = np.asarray
    order = np.arange(H).reshape(P, PHASES).T.reshape(-1)

    def chunked(w):
        w = a(w).T[order].reshape(HC, P, I)
        return np.concatenate([w[:, :, ic * P:ic * P + width(ic)].transpose(1, 0, 2).reshape(P, -1)
                               for ic in range(IC)], axis=1)

    def by_chunk(w):
        w = a(w)
        w = np.concatenate([w, np.zeros((IC * P - I,) + w.shape[1:], w.dtype)])
        return w.reshape(IC, P, -1).transpose(1, 0, 2).reshape(P, -1)

    def broadcast(w, n):
        return np.broadcast_to(a(w)[None, :], (n, len(w)))

    lr_a = np.stack([a(L0_ffn_gate_A)[order], a(L0_ffn_up_A)[order]], axis=1).reshape(HC, P, 2 * R).transpose(1, 0, 2)
    cond_pack = np.zeros((P, COND_COLS), np.float32)
    for at, w in zip(COND_AT, (a(cond_128).T, a(L0_cond_W0), a(L0_cond_W1), a(L0_cond_W2), a(L0_cond_b0)[:, None],
                               a(L0_cond_b1)[:, None], broadcast(L0_cond_b2, B))):
        cond_pack[:w.shape[0], at:at + w.shape[1]] = w
    w = a(L1_cond_weight)
    conv_w = np.zeros((S, PHASES, SHIFTS, PHASES, S), w.dtype)
    for c in range(S):
        same = slice(c // CG * CG, (c // CG + 1) * CG)
        for into in range(PHASES):
            for shift in range(SHIFTS):
                for of in range(PHASES):
                    tap = PHASES * (shift - 1) + into - of + PAD
                    if 0 <= tap < TAPS:
                        conv_w[c, into, shift, of, same] = w[same, c % CG, tap]
    row = np.arange(P)[:, None] % B
    batch_mask = np.concatenate([row % GB == np.arange(GB), row // GB == np.arange(GROUPS)],
                                axis=1).astype(np.float32)
    sel = (np.arange(P)[:, None] % R == np.arange(P)[None, :] % R).astype(np.float32)
    arrays = {
        "x": a(x).reshape(TOKENS, H)[:, order], "cond_pack": cond_pack,
        "cond_w": a(L0_cond_weight).reshape(EXPERTS, S * S), "bias_k": a(L0_cond_bias_k),
        "gate_q": chunked(L0_ffn_gate_q), "up_q": chunked(L0_ffn_up_q),
        "gate_s": by_chunk(L0_ffn_gate_scale), "up_s": by_chunk(L0_ffn_up_scale),
        "lr_a": lr_a.reshape(P, -1), "gate_b": np.tile(a(L0_ffn_gate_B), (4, 1)),
        "up_b": np.tile(a(L0_ffn_up_B), (4, 1)),
        "down_q": by_chunk(a(L0_ffn_down_q)[order].T), "down_s": broadcast(a(L0_ffn_down_scale)[order], P),
        "down_a": by_chunk(L0_ffn_down_A), "down_b": np.tile(a(L0_ffn_down_B)[:, order], (4, 1)),
        "conv_w": conv_w.reshape(P, -1), "ctx_w": a(L1_cond_c_weight).T,
        "fside": broadcast(fside_S_0, P),
        "ffn_w": a(L1_ffn_weight)[order][:, order].reshape(HC, P, H).transpose(1, 0, 2).reshape(P, -1),
        "batch_mask": batch_mask, "ident": np.eye(P, dtype=np.float32), "sel": sel,
    }
    arrays = {f"in_{k}": np.ascontiguousarray(v) for k, v in arrays.items()}
    nc = bacc.Bacc("TRN2", target_bir_lowering=False, num_devices=1, dynamic_dma_scratch_size=1024)
    aps = [nc.dram_tensor(k, v.shape, mybir.dt.from_np(v.dtype), kind="ExternalInput").ap()
           for k, v in arrays.items()]
    out = nc.dram_tensor("out", (TOKENS, H), F32, kind="ExternalOutput").ap()
    turned = nc.dram_tensor("turned", (GROUPS, 2, P, H), F32, kind="Internal").ap()
    build(nc, *aps, turned, out)
    r = run_bass_kernel_spmd(nc, [arrays], core_ids=[0])
    result = np.empty((TOKENS, H), np.float32)
    result[:, order] = r.results[0]["out"]
    return result.reshape(B, S, H)
```
